# Optimizing a Trainium2 kernel written in Bass

```python
import numpy as np
import jax
import jax.numpy as jnp

def _softmax(x, axis=-1):
    return jax.nn.softmax(x, axis=axis)

def _gelu(x):
    return jax.nn.gelu(x, approximate=True)

def _silu(x):
    return jax.nn.silu(x)

def _sigmoid(x):
    return jax.nn.sigmoid(x)

def _layernorm(x, axis=-1, eps=1e-05):
    m = jnp.mean(x, axis=axis, keepdims=True)
    v = jnp.var(x, axis=axis, keepdims=True)
    return (x - m) / jnp.sqrt(v + eps)

def _scatter_add(tgt, idx, src, axis=0):
    return tgt.at[idx].add(src)

def _segment_sum(src, seg, n):
    return jax.ops.segment_sum(src, seg, n)
kernel_name = 'mk_xattn_seq_d1_seqx_r8_0bb894'

def setup_inputs(seed: int=0):
    np.random.seed(seed)
    _w = jnp.asarray

    def _rec_inputs():
        import jax
        import jax.numpy as jnp
        _rk = jax.random.key(seed)
        x = -0.0002928 + 1 * jax.random.normal(jax.random.fold_in(_rk, 1), (128, 64, 128), jnp.float32)
        _lenS = 64 - jax.random.randint(jax.random.fold_in(_rk, 7), (128,), 0, max(1, 64 // 4) + 1, jnp.int32)
        _lenS2 = 64 - jax.random.randint(jax.random.fold_in(_rk, 8), (128,), 0, max(1, 64 // 4) + 1, jnp.int32)
        _ctx_768P = jax.random.normal(jax.random.fold_in(_rk, 11), (128, 16, 96), jnp.float32)
        _ctx_768c = jax.random.dirichlet(jax.random.fold_in(_rk, 511), 0.3 * jnp.ones((16,), jnp.float32), (128, 64))
        _ctx_768t = jnp.einsum('bsk,bkd->bsd', _ctx_768c, _ctx_768P)
        _ctx_768t = _ctx_768t * jax.lax.rsqrt(jnp.mean(jnp.square(_ctx_768t)) + 1e-12) * 0.953939
        ctx_768 = -0.00423632 + 0.9977 * (_ctx_768t + 0.3 * jax.random.normal(jax.random.fold_in(_rk, 611), (128, 64, 96), jnp.float32))
        return (x, ctx_768)
    x, ctx_768 = _rec_inputs()

    def _L0_xattn_setup():
        import jax, jax.numpy as jnp
        import numpy as np
        DIM, HEADS, DHEAD, CTX_DIM = (128, 16, 64, 96)
        INNER = HEADS * DHEAD
        FF_HID = 4 * DIM
        EPS = 1e-05

        def _ln(x, g, b):
            mu = jnp.mean(x, axis=-1, keepdims=True)
            var = jnp.mean(jnp.square(x - mu), axis=-1, keepdims=True)
            return (x - mu) * jax.lax.rsqrt(var + EPS) * g + b

        def _attn(x, ctx, Wq, Wk, Wv, Wo, bo):
            b, n, _ = x.shape
            m = ctx.shape[1]
            q = (x @ Wq).reshape(b, n, HEADS, DHEAD)
            k = (ctx @ Wk).reshape(b, m, HEADS, DHEAD)
            v = (ctx @ Wv).reshape(b, m, HEADS, DHEAD)
            scale = DHEAD ** (-0.5)
            sim = jnp.einsum('bihd,bjhd->bhij', q, k) * scale
            attn = jax.nn.softmax(sim, axis=-1)
            out = jnp.einsum('bhij,bjhd->bihd', attn, v).reshape(b, n, INNER)
            return out @ Wo + bo
        key = jax.random.key(seed)
        ks = jax.random.split(key, 24)

        def w(k, shape, fan_in):
            return jax.random.normal(k, shape, jnp.float32) * fan_in ** (-0.5)
        inp = {'x': jax.random.normal(ks[0], (2, 256, DIM), jnp.float32), 'context': jax.random.normal(ks[1], (2, 77, CTX_DIM), jnp.float32), 'Wq1': w(ks[2], (DIM, INNER), DIM), 'Wk1': w(ks[3], (DIM, INNER), DIM), 'Wv1': w(ks[4], (DIM, INNER), DIM), 'Wo1': w(ks[5], (INNER, DIM), INNER), 'bo1': jnp.zeros((DIM,), jnp.float32), 'Wq2': w(ks[6], (DIM, INNER), DIM), 'Wk2': w(ks[7], (CTX_DIM, INNER), CTX_DIM), 'Wv2': w(ks[8], (CTX_DIM, INNER), CTX_DIM), 'Wo2': w(ks[9], (INNER, DIM), INNER), 'bo2': jnp.zeros((DIM,), jnp.float32), 'Wp': w(ks[10], (DIM, 2 * FF_HID), DIM), 'bp': jnp.zeros((2 * FF_HID,), jnp.float32), 'W2': w(ks[11], (FF_HID, DIM), FF_HID), 'b2': jnp.zeros((DIM,), jnp.float32), 'g1': jnp.ones((DIM,), jnp.float32), 'be1': jnp.zeros((DIM,), jnp.float32), 'g2': jnp.ones((DIM,), jnp.float32), 'be2': jnp.zeros((DIM,), jnp.float32), 'g3': jnp.ones((DIM,), jnp.float32), 'be3': jnp.zeros((DIM,), jnp.float32)}
        return inp
    _L0_xattn_all = _L0_xattn_setup()
    _L0_xattn_in = {k: v for k, v in _L0_xattn_all.items() if k in ('Wq1', 'Wk1', 'Wv1', 'Wo1', 'bo1', 'Wq2', 'Wk2', 'Wv2', 'Wo2', 'bo2', 'Wp', 'bp', 'W2', 'b2', 'g1', 'be1', 'g2', 'be2', 'g3', 'be3')}
    del _L0_xattn_all
    return {'x': x, 'ctx_768': ctx_768, 'L0_xattn_Wq1': _L0_xattn_in['Wq1'], 'L0_xattn_Wk1': _L0_xattn_in['Wk1'], 'L0_xattn_Wv1': _L0_xattn_in['Wv1'], 'L0_xattn_Wo1': _L0_xattn_in['Wo1'], 'L0_xattn_bo1': _L0_xattn_in['bo1'], 'L0_xattn_Wq2': _L0_xattn_in['Wq2'], 'L0_xattn_Wk2': _L0_xattn_in['Wk2'], 'L0_xattn_Wv2': _L0_xattn_in['Wv2'], 'L0_xattn_Wo2': _L0_xattn_in['Wo2'], 'L0_xattn_bo2': _L0_xattn_in['bo2'], 'L0_xattn_Wp': _L0_xattn_in['Wp'], 'L0_xattn_bp': _L0_xattn_in['bp'], 'L0_xattn_W2': _L0_xattn_in['W2'], 'L0_xattn_b2': _L0_xattn_in['b2'], 'L0_xattn_g1': _L0_xattn_in['g1'], 'L0_xattn_be1': _L0_xattn_in['be1'], 'L0_xattn_g2': _L0_xattn_in['g2'], 'L0_xattn_be2': _L0_xattn_in['be2'], 'L0_xattn_g3': _L0_xattn_in['g3'], 'L0_xattn_be3': _L0_xattn_in['be3']}

def reference(x, ctx_768, L0_xattn_Wq1, L0_xattn_Wk1, L0_xattn_Wv1, L0_xattn_Wo1, L0_xattn_bo1, L0_xattn_Wq2, L0_xattn_Wk2, L0_xattn_Wv2, L0_xattn_Wo2, L0_xattn_bo2, L0_xattn_Wp, L0_xattn_bp, L0_xattn_W2, L0_xattn_b2, L0_xattn_g1, L0_xattn_be1, L0_xattn_g2, L0_xattn_be2, L0_xattn_g3, L0_xattn_be3):
    import jax
    import jax.numpy as jnp

    def _L0_xattn_ref(x, context, Wq1, Wk1, Wv1, Wo1, bo1, Wq2, Wk2, Wv2, Wo2, bo2, Wp, bp, W2, b2, g1, be1, g2, be2, g3, be3):
        import jax, jax.numpy as jnp
        import numpy as np
        DIM, HEADS, DHEAD, CTX_DIM = (128, 16, 64, 96)
        INNER = HEADS * DHEAD
        FF_HID = 4 * DIM
        EPS = 1e-05

        def _ln(x, g, b):
            mu = jnp.mean(x, axis=-1, keepdims=True)
            var = jnp.mean(jnp.square(x - mu), axis=-1, keepdims=True)
            return (x - mu) * jax.lax.rsqrt(var + EPS) * g + b

        def _attn(x, ctx, Wq, Wk, Wv, Wo, bo):
            b, n, _ = x.shape
            m = ctx.shape[1]
            q = (x @ Wq).reshape(b, n, HEADS, DHEAD)
            k = (ctx @ Wk).reshape(b, m, HEADS, DHEAD)
            v = (ctx @ Wv).reshape(b, m, HEADS, DHEAD)
            scale = DHEAD ** (-0.5)
            sim = jnp.einsum('bihd,bjhd->bhij', q, k) * scale
            attn = jax.nn.softmax(sim, axis=-1)
            out = jnp.einsum('bhij,bjhd->bihd', attn, v).reshape(b, n, INNER)
            return out @ Wo + bo
        h = _ln(x, g1, be1)
        x = _attn(h, h, Wq1, Wk1, Wv1, Wo1, bo1) + x
        h = _ln(x, g2, be2)
        x = _attn(h, context, Wq2, Wk2, Wv2, Wo2, bo2) + x
        h = _ln(x, g3, be3)
        y = h @ Wp + bp
        a, gate = (y[..., :FF_HID], y[..., FF_HID:])
        x = a * jax.nn.gelu(gate, approximate=False) @ W2 + b2 + x
        return x
    x = _L0_xattn_ref(x, ctx_768, L0_xattn_Wq1, L0_xattn_Wk1, L0_xattn_Wv1, L0_xattn_Wo1, L0_xattn_bo1, L0_xattn_Wq2, L0_xattn_Wk2, L0_xattn_Wv2, L0_xattn_Wo2, L0_xattn_bo2, L0_xattn_Wp, L0_xattn_bp, L0_xattn_W2, L0_xattn_b2, L0_xattn_g1, L0_xattn_be1, L0_xattn_g2, L0_xattn_be2, L0_xattn_g3, L0_xattn_be3)
    return x

_drawn_inputs = setup_inputs


def setup_inputs(seed=0):
    import zlib

    import numpy as np

    out = dict(_drawn_inputs(seed))
    spreads = {'L0_xattn_bo1': (0.0, 0.1),
     'L0_xattn_bo2': (0.0, 0.1),
     'L0_xattn_bp': (0.0, 0.1),
     'L0_xattn_b2': (0.0, 0.1),
     'L0_xattn_g1': (1.0, 0.2),
     'L0_xattn_be1': (0.0, 0.1),
     'L0_xattn_g2': (1.0, 0.2),
     'L0_xattn_be2': (0.0, 0.325),
     'L0_xattn_g3': (1.0, 0.2),
     'L0_xattn_be3': (0.0, 0.1)}
    factors = {}
    for name, (base, spread) in spreads.items():
        noise = np.random.default_rng([zlib.crc32(name.encode()), seed]).standard_normal(out[name].shape)
        drawn = base * np.exp(spread * noise) if base else spread * noise
        out[name] = jnp.asarray(drawn.astype(out[name].dtype))
    for name, factor in factors.items():
        out[name] = (out[name] * factor).astype(out[name].dtype)
    return out
```

```python
from contextlib import ExitStack

import concourse.bass as bass
from concourse import mybir

ALU = mybir.AluOpType
ACT = mybir.ActivationFunctionType
F32 = mybir.dt.float32
F32R = mybir.dt.float32r
AX_X = mybir.AxisListType.X

P = 128
SEQ = 64
DH = 64
HEADS = 16
CTX = 96
FF = 512
EPS = 1e-5
SCALE = DH ** -0.5

TOK = 512
PAIRS = TOK // P
HALF = HEADS // 2
HP = HALF // 2
STEPS = 2 * 2 * PAIRS
BLOCKS = STEPS // PAIRS
FFC = FF // P
LN1_AT, LN2_AT, LN3_AT = PAIRS, 2 * PAIRS, 0
FF_AT = PAIRS
GELU_AT = FF_AT + FFC
DOWN_AT = 11


def wait(eng, sem, value):
    if not (isinstance(value, int) and value <= 0):
        eng.wait_ge(sem, value)


def f32(ap):
    return ap.bitcast(F32)


def block_kernel(nc, x, ctxT, wqT, wkT, wv, wo, bo, wp, bp, w2, b2, ln_g, ln_b, out):
    n_tiles = x.shape[0] // TOK
    assert ctxT.shape == (n_tiles, CTX, TOK) and n_tiles >= 4

    with ExitStack() as stack:
        def sb(name, shape, dt=F32):
            return stack.enter_context(nc.sbuf_tensor(name, shape, dt))

        def pb(name, shape):
            return stack.enter_context(nc.psum_tensor(name, shape, F32))

        def sem(name):
            return stack.enter_context(nc.semaphore(name))

        m_hi = [sb(f"m{a}_hi", [P, HEADS, P], F32R) for a in (1, 2)]
        m_lo = [sb(f"m{a}_lo", [P, HEADS, P], F32R) for a in (1, 2)]
        wv_hi = [sb(f"wv{a}_hi", [P, HEADS * DH], F32R) for a in (1, 2)]
        wv_lo = [sb(f"wv{a}_lo", [P, HEADS * DH], F32R) for a in (1, 2)]
        wo_sb = [sb(f"wo{a}_sb", [P, HEADS // 2, P]) for a in (1, 2)]
        wp_hi = sb("wp_hi", [P, 2 * FF], F32R)
        wp_lo = sb("wp_lo", [P, 2 * FF], F32R)
        w2_sb = sb("w2_sb", [P, FFC, P])
        bo_sb = [sb(f"bo{a}_sb", [P, P]) for a in (1, 2)]
        b2_sb = sb("b2_sb", [P, P])
        bp_sb = sb("bp_sb", [P, 2 * FFC])
        g_sb = sb("g_sb", [P, 3])
        be_sb = sb("be_sb", [P, 3])
        ident = sb("ident", [P, P])
        minus_half = sb("minus_half", [P, 1])
        eps_sb = sb("eps_sb", [P, 1])

        x_in = sb("x_in", [P, PAIRS, P])
        x_bo1 = sb("x_bo1", [P, PAIRS, P])
        x1 = sb("x1", [P, PAIRS, P])
        x1_bo2 = sb("x1_bo2", [P, PAIRS, P])
        x2 = sb("x2", [P, PAIRS, P])
        x2_b2 = sb("x2_b2", [P, PAIRS, P])
        y_out = sb("y_out", [P, PAIRS, P])
        z = sb("z", [P, 2, P])
        stats = sb("stats", [P, 6])
        mean_var = [sb(f"mean_var{k}", [P, 2, 2]) for k in (1, 2, 3)]
        var_eps = [sb(f"var_eps{k}", [P, 2]) for k in (1, 2, 3)]
        rstd = [sb(f"rstd{k}", [P, 2]) for k in (1, 2, 3)]

        h1, h2, h3 = (sb(f"h{k}", [P, TOK]) for k in (1, 2, 3))
        h1_hi, h1_lo = sb("h1_hi", [P, TOK], F32R), sb("h1_lo", [P, TOK], F32R)
        h3_hi, h3_lo = sb("h3_hi", [P, TOK], F32R), sb("h3_lo", [P, TOK], F32R)
        c_in = sb("c_in", [P, TOK])
        c_hi, c_lo = sb("c_hi", [P, TOK], F32R), sb("c_lo", [P, TOK], F32R)
        gate = sb("gate", [P, FFC, TOK])
        up = sb("up", [P, FFC, TOK])

        keys = sb("keys", [P, 2, HALF, TOK])
        values = sb("values", [P, 2, PAIRS, HALF * DH])
        probs = sb("probs", [P, 4, HP, P])
        probsT = sb("probsT", [P, 2, HP, P])
        attnT = sb("attnT", [P, 2, HP, 2, SEQ])
        row_max = sb("row_max", [P, 2, 2 * HP])
        row_sum = sb("row_sum", [P, 2, 2 * HP])
        row_inv = sb("row_inv", [P, 2, 2 * HP])

        scores_ps = pb("scores_ps", [P, 512])
        turn_ps = pb("turn_ps", [P, HP, P])
        attn_ps = pb("attn_ps", [P, 2, 512])
        key_ps = [pb(f"key_ps{i}", [P, 512]) for i in range(2)]
        value_ps = pb("value_ps", [P, 512])
        ln_ps = pb("ln_ps", [P, 512])
        proj_ps = attn_ps[:, 0, 256:384]
        down_ps = ln_ps[:, 256:384]

        raw = keys[:, :, :, :].rearrange("p a h t -> p (a h t)")
        W = HEADS * DH
        wqT_raw = [raw[:, i * W:(i + 1) * W].rearrange("p (c n) -> p c n", n=P) for i in (0, 1)]
        wk1T_raw = raw[:, 2 * W:3 * W].rearrange("p (c n) -> p c n", n=P)
        wk2T_raw = raw[:, 3 * W:3 * W + HEADS // 2 * CTX].rearrange("p (c n) -> p c n", n=CTX)
        wkT_raw = [wk1T_raw, wk2T_raw]
        wv_raw = [raw[:, 4 * W:5 * W], raw[:, 5 * W:6 * W]]
        wp_raw = raw[:, 6 * W:7 * W]
        banks = [scores_ps[:, :], turn_ps[:, :, :].rearrange("p a b -> p (a b)"), attn_ps[:, 0, :],
                 attn_ps[:, 1, :], key_ps[0][:, :], key_ps[1][:, :], value_ps[:, :], ln_ps[:, :]]
        cdim = [P, CTX]

        qk_loaded = sem("qk_loaded")
        vp_loaded = sem("vp_loaded")
        small_loaded = sem("small_loaded")
        out_w_loaded = sem("out_w_loaded")
        const_made = sem("const_made")
        m_full = sem("m_full")
        w_hi_done = sem("w_hi_done")
        w_lo_done = sem("w_lo_done")
        x_loaded = sem("x_loaded")
        ctx_loaded = sem("ctx_loaded")
        stored = sem("stored")
        stat_done = [sem(f"stat_done{k}") for k in (1, 2, 3)]
        raw_stat = sem("raw_stat")
        eps_added = sem("eps_added")
        rstd_done = [sem(f"rstd_done{k}") for k in (1, 2, 3)]
        z_done = [sem(f"z_done{k}") for k in (1, 2, 3)]
        turned = [sem(f"ln_turned{k}") for k in (1, 2, 3)]
        h_done = [sem(f"h_done{k}") for k in (1, 2, 3)]
        hi_done = [sem(f"hi_done{k}") for k in (1, 2, 3)]
        lo_done = [sem(f"lo_done{k}") for k in (1, 2, 3)]
        c_hi_done = sem("c_hi_done")
        c_lo_done = sem("c_lo_done")
        key_full = sem("key_full")
        key_done = sem("key_done")
        value_full = sem("value_full")
        value_done = sem("value_done")
        scores_full = sem("scores_full")
        max_done = sem("max_done")
        sub_done = sem("sub_done")
        exp_done = sem("exp_done")
        sum_done = sem("sum_done")
        inv_done = sem("inv_done")
        probs_done = sem("probs_done")
        turn_full = sem("turn_full")
        probsT_done = sem("probsT_done")
        attn_full = sem("attn_full")
        attnT_done = sem("attnT_done")
        proj_full = sem("proj_full")
        res_done = sem("res_done")
        x_bo1_done = sem("x_bo1_done")
        x1_bo2_done = sem("x1_bo2_done")
        x2_b2_done = sem("x2_b2_done")
        gate_full = sem("gate_full")
        gate_done = sem("gate_done")
        up_full = sem("up_full")
        up_done = sem("up_done")
        gelu_done = sem("gelu_done")
        gated = sem("gated")
        down_full = sem("down_full")
        out_done = sem("out_done")

        N_QK, N_VP, N_SMALL, N_OUT_W = 4, 3, 6, 3
        W_PARTS = 8 + 3

        SMALL = 16 * N_SMALL
        def windows(eng, window):
            window(-1, False, False, True)
            window(0, False, True, True)
            window(1, True, True, True)
            with eng.Fori(2, n_tiles - 1) as T:
                window(T, True, True, True)
            window(n_tiles - 1, True, True, False)
            window(n_tiles, True, False, False)

        def ln_item(s, prev, cur, nxt):
            for k, at, off, on in ((1, LN1_AT, 1, nxt), (2, LN2_AT, 0, cur), (3, LN3_AT, -1, prev)):
                if on and at <= s < at + PAIRS:
                    return k, s - at, off
            return None

        def ln_item_next(s, prev, cur, nxt):
            if s == STEPS - 1:
                return (3, 0, 0) if cur else None
            return ln_item(s + 1, prev, cur, nxt)

        def eps_count(T, s, prev, cur, nxt):
            in_window = sum(ln_item_next(q, prev, cur, nxt) is not None for q in range(s + 1))
            if isinstance(T, int):
                before = {-1: 0, 0: PAIRS}.get(T, PAIRS + (2 * PAIRS + 1) + 3 * PAIRS * (T - 1))
                if T == n_tiles:
                    before -= PAIRS
            else:
                before = PAIRS + (2 * PAIRS + 1) - 3 * PAIRS + 3 * PAIRS * T
            return before + in_window

        block = stack.enter_context(nc.Block())

        @block.sync
        def _(sp):
            for a in range(2):
                sp.dma_start(wqT_raw[a], wqT[a].rearrange("(c p) n -> p c n", p=P)).then_inc(qk_loaded, 16)
                sp.dma_start(wkT_raw[a], wkT[a].rearrange("(c p) n -> p c n", p=P)).then_inc(qk_loaded, 16)

            def load_x(t):
                wait(sp, z_done[0], PAIRS * t)
                wait(sp, x_bo1_done, PAIRS * t)
                sp.dma_start(x_in[:, :, :], x[bass.ts(t, TOK), :].rearrange("(c p) d -> p c d", p=P))\
                    .then_inc(x_loaded, 16)

            def load_ctx(t):
                wait(sp, c_lo_done, t)
                sp.dma_start(c_in[0:CTX, :], ctxT[bass.ts(t, 1), :, :].rearrange("a c t -> c (a t)"))\
                    .then_inc(ctx_loaded, 16)

            def store(t):
                sp.wait_ge(out_done, PAIRS * t + PAIRS)
                sp.dma_start(out[bass.ts(t, TOK), :].rearrange("(c p) d -> p c d", p=P), y_out[:, :, :])\
                    .then_inc(stored, 16)

            for t in range(2):
                load_x(t)
                load_ctx(t)
            with sp.Fori(2, n_tiles) as t:
                load_x(t)
                load_ctx(t)
                store(t - 2)
            for t in (n_tiles - 2, n_tiles - 1):
                store(t)
            sp.wait_ge(stored, 16 * n_tiles)

        @block.gpsimd
        def _(pool):
            pool.memset(minus_half[:, :], -0.5).then_inc(const_made, 1)
            pool.memset(ident[:, :], 0.0).then_inc(const_made, 1)
            pool.memset(eps_sb[:, :], EPS).then_inc(const_made, 1)
            pool.wait_ge(const_made, 3)
            pool.affine_select(out=ident[:, :], in_=ident[:, :], compare_op=ALU.not_equal, fill=1.0, base=0,
                               pattern=[[-1, P]], channel_multiplier=1).then_inc(const_made, 1)
            pool.wait_ge(const_made, 4)
            pool.wait_ge(small_loaded, SMALL)

            def window(T, prev, cur, nxt):
                for s in range(STEPS):
                    G = STEPS * T + s
                    if item := ln_item_next(s, prev, cur, nxt):
                        k, i, off = item
                        n = PAIRS * (T + off) + i
                        wait(pool, stat_done[k - 1], n + 1)
                        slot = i % 2
                        pool.tensor_tensor(var_eps[k - 1][:, slot:slot + 1], mean_var[k - 1][:, slot, 1:2],
                                           eps_sb[:, :], ALU.add).then_inc(eps_added, 1)
                        wait(pool, eps_added, eps_count(T, s, prev, cur, nxt))
                        pool.tensor_tensor(rstd[k - 1][:, slot:slot + 1], var_eps[k - 1][:, slot:slot + 1],
                                           minus_half[:, :], ALU.pow).then_inc(rstd_done[k - 1], 1)
                    if prev and s < PAIRS:
                        n = PAIRS * (T - 1) + s
                        cols = slice(s * P, (s + 1) * P)
                        wait(pool, hi_done[2], n + 1)
                        pool.tensor_tensor(h3_lo[:, cols], h3[:, cols], f32(h3_hi[:, cols]), ALU.subtract)\
                            .then_inc(lo_done[2], 1)
                        wait(pool, res_done, STEPS * (T - 1) + 3 * PAIRS + s + 1)
                        pool.tensor_tensor(x2_b2[:, s, :], x2[:, s, :], b2_sb[:, :], ALU.add)\
                            .then_inc(x2_b2_done, 1)
                    if nxt and LN1_AT <= s < LN1_AT + PAIRS:
                        i = s - LN1_AT
                        wait(pool, x_loaded, 16 * (T + 2))
                        wait(pool, res_done, STEPS * T + i + 1)
                        pool.tensor_tensor(x_bo1[:, i, :], x_in[:, i, :], bo_sb[0][:, :], ALU.add)\
                            .then_inc(x_bo1_done, 1)
                    if nxt and LN1_AT < s <= LN1_AT + PAIRS:
                        i = s - LN1_AT - 1
                        cols = slice(i * P, (i + 1) * P)
                        wait(pool, hi_done[0], PAIRS * (T + 1) + i + 1)
                        pool.tensor_tensor(h1_lo[:, cols], h1[:, cols], f32(h1_hi[:, cols]), ALU.subtract)\
                            .then_inc(lo_done[0], 1)
                    if cur and s == 2:
                        wait(pool, c_hi_done, T + 1)
                        pool.tensor_tensor(c_lo[0:CTX, :], c_in[0:CTX, :], f32(c_hi[0:CTX, :]), ALU.subtract)\
                            .then_inc(c_lo_done, 1)
                    if cur and LN2_AT <= s < LN2_AT + PAIRS:
                        i = s - LN2_AT
                        wait(pool, res_done, STEPS * T + PAIRS + i + 1)
                        pool.tensor_tensor(x1_bo2[:, i, :], x1[:, i, :], bo_sb[1][:, :], ALU.add)\
                            .then_inc(x1_bo2_done, 1)
                    if prev and s == GELU_AT:
                        wait(pool, gelu_done, T)
                        wait(pool, up_done, FFC * T)
                        for j in range(FFC):
                            pool.tensor_tensor(up[:, j, :], up[:, j, :], gate[:, j, :], ALU.mult)\
                                .then_inc(gated, 1)

            windows(pool, window)

        @block.scalar
        def _(act):
            for a in range(2):
                act.dma_start(wv_raw[a][0:cdim[a], :], wv[a]).then_inc(vp_loaded, 16)
            act.dma_start(wp_raw, wp).then_inc(vp_loaded, 16)
            act.dma_start(g_sb[:, :], ln_g).then_inc(small_loaded, 16)
            act.dma_start(be_sb[:, :], ln_b).then_inc(small_loaded, 16)
            act.dma_start(bp_sb[:, :], bp).then_inc(small_loaded, 16)
            for dst, src in ((bo_sb[0], bo[0]), (bo_sb[1], bo[1]), (b2_sb, b2)):
                act.dma_start(dst[:, :], src.partition_broadcast(P)).then_inc(small_loaded, 16)
            for a in range(2):
                act.dma_start(wo_sb[a][:, :, :], wo[a].rearrange("(c p) n -> p c n", p=P))\
                    .then_inc(out_w_loaded, 16)
            act.dma_start(w2_sb[:, :, :], w2.rearrange("(c p) n -> p c n", p=P)).then_inc(out_w_loaded, 16)

            act.wait_ge(m_full, 1)
            for n in range(8):
                a, par, c = n // 4, n // 2 % 2, n % 2
                act.wait_ge(m_full, n + 1)
                heads = m_hi[a][0:cdim[a], :, :].rearrange("p (c q) n -> p c q n", q=2)
                act.activation(heads[:, 4 * c:4 * c + 4, par, :],
                               banks[n][0:cdim[a], :].rearrange("p (c n) -> p c n", n=P),
                               ACT.Copy, scale=SCALE).then_inc(w_hi_done, 1)
            act.wait_ge(vp_loaded, 16 * N_VP)
            for a in range(2):
                act.activation(wv_hi[a][0:cdim[a], :], wv_raw[a][0:cdim[a], :], ACT.Copy).then_inc(w_hi_done, 1)
            act.activation(wp_hi[:, :], wp_raw, ACT.Copy).then_inc(w_hi_done, 1)
            act.wait_ge(small_loaded, SMALL)

            def window(T, prev, cur, nxt):
                for s in range(STEPS):
                    G = STEPS * T + s
                    lagged = cur if s >= 2 else prev
                    if lagged:
                        wait(act, turn_full, G - 1)
                        wait(act, attn_full, G - 3)
                        act.activation(probsT[:, s % 2, :, :], turn_ps[:, :, :], ACT.Copy)\
                            .then_inc(probsT_done, 1)
                    j = G + PAIRS
                    projecting = cur if s < STEPS - PAIRS else nxt
                    buf = (s // PAIRS + 1) % 2
                    if projecting:
                        if s % PAIRS == 0:
                            wait(act, scores_full, j - PAIRS)
                        for u in range(2):
                            wait(act, key_full, 2 * j + u + 1)
                            act.activation(keys[:, buf, 2 * (s % PAIRS) + u, :], key_ps[u][:, :], ACT.Copy)\
                                .then_inc(key_done, 1)
                    if prev and s < PAIRS:
                        cols = slice(s * P, (s + 1) * P)
                        wait(act, h_done[2], PAIRS * (T - 1) + s + 1)
                        act.activation(h3_hi[:, cols], h3[:, cols], ACT.Copy).then_inc(hi_done[2], 1)
                    if nxt and LN1_AT < s <= LN1_AT + PAIRS:
                        i = s - LN1_AT - 1
                        cols = slice(i * P, (i + 1) * P)
                        wait(act, h_done[0], PAIRS * (T + 1) + i + 1)
                        act.activation(h1_hi[:, cols], h1[:, cols], ACT.Copy).then_inc(hi_done[0], 1)
                    if lagged:
                        wait(act, attn_full, G - 1)
                        wait(act, proj_full, G - 3)
                        act.activation(attnT[:, s % 2, :, :, :].rearrange("p h b q -> p b h q"),
                                       attn_ps[:, :, 0:HP * SEQ].rearrange("p b (h q) -> p b h q", q=SEQ),
                                       ACT.Copy).then_inc(attnT_done, 1)
                    if projecting:
                        wait(act, value_full, j + 1)
                        wait(act, attn_full, j - 2 * PAIRS + 1)
                        act.activation(values[:, buf, s % PAIRS, :], value_ps[:, :], ACT.Copy)\
                            .then_inc(value_done, 1)
                    if cur:
                        wait(act, sub_done, G + 1)
                        e = probs[:, s % 4, :, :]
                        act.activation(e, e, ACT.Exp).then_inc(exp_done, 1)
                    if cur and s == 1:
                        wait(act, ctx_loaded, 16 * (T + 1))
                        act.activation(c_hi[0:CTX, :], c_in[0:CTX, :], ACT.Copy).then_inc(c_hi_done, 1)
                    if prev and FF_AT <= s < FF_AT + FFC:
                        i = s - FF_AT
                        wait(act, gate_full, FFC * (T - 1) + i + 1)
                        wait(act, gated, FFC * (T - 1))
                        act.activation(gate[:, i, :], key_ps[0][:, :], ACT.Identity,
                                       bias=bp_sb[:, FFC + i:FFC + i + 1]).then_inc(gate_done, 1)
                    if prev and s == GELU_AT:
                        wait(act, gate_done, FFC * T)
                        act.activation(gate[:, :, :], gate[:, :, :], ACT.Gelu).then_inc(gelu_done, 1)

            windows(act, window)

        @block.vector
        def _(dve):
            for n in range(8):
                a, par, c = n // 4, n // 2 % 2, n % 2
                dve.wait_ge(w_hi_done, n + 1)
                hi = f32(m_hi[a][0:cdim[a], :, :]).rearrange("p (c q) n -> p c q n", q=2)
                lo = m_lo[a][0:cdim[a], :, :].rearrange("p (c q) n -> p c q n", q=2)
                dve.scalar_tensor_tensor(out=lo[:, 4 * c:4 * c + 4, par, :],
                                         in0=banks[n][0:cdim[a], :].rearrange("p (c n) -> p c n", n=P),
                                         scalar=SCALE, in1=hi[:, 4 * c:4 * c + 4, par, :],
                                         op0=ALU.mult, op1=ALU.subtract).then_inc(w_lo_done, 1)
            for n, (dst, src, hi, rows) in enumerate(((wv_lo[0], wv_raw[0], wv_hi[0], P),
                                                      (wv_lo[1], wv_raw[1], wv_hi[1], CTX),
                                                      (wp_lo, wp_raw, wp_hi, P))):
                dve.wait_ge(w_hi_done, 9 + n)
                dve.tensor_tensor(dst[0:rows, :], src[0:rows, :], f32(hi[0:rows, :]), ALU.subtract)\
                    .then_inc(w_lo_done, 1)
            dve.wait_ge(small_loaded, SMALL)

            def ln_out(k, i, off, T, h):
                wait(dve, turned[k - 1], PAIRS * (T + off) + i + 1)
                dve.tensor_scalar(h[:, i * P:(i + 1) * P], ln_ps[:, 0:P], g_sb[:, k - 1:k], be_sb[:, k - 1:k],
                                  ALU.mult, ALU.add).then_inc(h_done[k - 1], 1)

            def window(T, prev, cur, nxt):
                for s in range(STEPS):
                    G = STEPS * T + s
                    if cur if s >= 3 else prev:
                        q = (s - 3) % STEPS
                        t = T if s >= 3 else T - 1
                        i = q % PAIRS
                        wait(dve, proj_full, G - 2)
                        if q // PAIRS == 0:
                            wait(dve, x_bo1_done, PAIRS * t + i + 1)
                            wait(dve, x1_bo2_done, PAIRS * (t - 1) + i + 1)
                            dst, src = x1[:, i, :], x_bo1[:, i, :]
                        elif q // PAIRS == 1:
                            dst, src = x1[:, i, :], x1[:, i, :]
                        elif q // PAIRS == 2:
                            wait(dve, x1_bo2_done, PAIRS * t + i + 1)
                            wait(dve, x2_b2_done, PAIRS * (t - 1) + i + 1)
                            dst, src = x2[:, i, :], x1_bo2[:, i, :]
                        else:
                            dst, src = x2[:, i, :], x2[:, i, :]
                        if q // PAIRS % 2:
                            wait(dve, res_done, G - 3 - PAIRS + 1)
                        dve.tensor_tensor(dst, proj_ps, src, ALU.add).then_inc(res_done, 1)
                    if prev and DOWN_AT < s <= DOWN_AT + PAIRS:
                        i = s - DOWN_AT - 1
                        wait(dve, down_full, PAIRS * (T - 1) + i + 1)
                        wait(dve, x2_b2_done, PAIRS * (T - 1) + i + 1)
                        if i == 0:
                            wait(dve, stored, 16 * (T - 1))
                        dve.tensor_tensor(y_out[:, i, :], down_ps, x2_b2[:, i, :], ALU.add).then_inc(out_done, 1)
                    item = ln_item(s, prev, cur, nxt)
                    if item and item[0] != 1:
                        ln_out(*item, T, h2 if item[0] == 2 else h3)
                    after = ln_item_next(s, prev, cur, nxt)
                    if after:
                        k, i, off = after
                        n = PAIRS * (T + off) + i
                        src = (x_in, x1, x2)[k - 1][:, i, :]
                        if k == 1:
                            wait(dve, x_loaded, 16 * (T + 2))
                        else:
                            wait(dve, res_done, G - 2)
                        dve.bn_stats(stats[:, :], src).then_inc(raw_stat, 1)
                    if cur if s >= 1 else prev:
                        e = probs[:, (s - 1) % 4, :, :].rearrange("p h (b k) -> p (h b) k", k=SEQ)
                        r = (s - 1) % 2
                        wait(dve, exp_done, G)
                        if after:
                            wait(dve, raw_stat, eps_count(T, s, prev, cur, nxt))
                        dve.tensor_reduce(row_sum[:, r, :], e, AX_X, ALU.add).then_inc(sum_done, 1)
                    elif after:
                        wait(dve, raw_stat, eps_count(T, s, prev, cur, nxt))
                    if after:
                        dve.bn_aggr(mean_var[k - 1][:, i % 2, :], stats[:, :]).then_inc(stat_done[k - 1], 1)
                    if cur if s >= 1 else prev:
                        wait(dve, sum_done, G)
                        dve.reciprocal(row_inv[:, r, :], row_sum[:, r, :]).then_inc(inv_done, 1)
                        wait(dve, inv_done, G)
                        dve.tensor_tensor(e, e, row_inv[:, r, :].unsqueeze(2).to_broadcast([P, 2 * HP, SEQ]),
                                          ALU.mult).then_inc(probs_done, 1)
                    if after:
                        wait(dve, rstd_done[k - 1], n + 1)
                        if i >= 2:
                            wait(dve, turned[k - 1], n - 1)
                        dve.tensor_scalar(z[:, i % 2, :], src, mean_var[k - 1][:, i % 2, 0:1],
                                          rstd[k - 1][:, i % 2:i % 2 + 1], ALU.subtract, ALU.mult)\
                            .then_inc(z_done[k - 1], 1)
                    if cur:
                        sc = scores_ps[:, :].rearrange("p (g k) -> p g k", k=SEQ)
                        e = probs[:, s % 4, :, :].rearrange("p h (b k) -> p (h b) k", k=SEQ)
                        r = s % 2
                        wait(dve, scores_full, G + 1)
                        dve.tensor_reduce(row_max[:, r, :], sc, AX_X, ALU.max).then_inc(max_done, 1)
                        wait(dve, max_done, G + 1)
                        wait(dve, turn_full, G - 3)
                        dve.tensor_tensor(e, sc, row_max[:, r, :].unsqueeze(2).to_broadcast([P, 2 * HP, SEQ]),
                                          ALU.subtract).then_inc(sub_done, 1)
                    if item and item[0] == 1:
                        ln_out(*item, T, h1)
                    if prev and FF_AT <= s < FF_AT + FFC:
                        i = s - FF_AT
                        wait(dve, up_full, FFC * (T - 1) + i + 1)
                        dve.tensor_scalar(up[:, i, :], key_ps[1][:, :], bp_sb[:, i:i + 1], None, ALU.add)\
                            .then_inc(up_done, 1)

            windows(dve, window)

        @block.tensor
        def _(pe):
            pe.wait_ge(qk_loaded, 16 * N_QK)
            for n in range(8):
                a, par, c = n // 4, n // 2 % 2, n % 2
                rows = slice(par * DH, (par + 1) * DH)
                for q in range(4):
                    mm = pe.matmul(banks[n][0:cdim[a], q * P:(q + 1) * P], wkT_raw[a][rows, 4 * c + q, :],
                                   wqT_raw[a][rows, 4 * c + q, :], start=True, stop=True)
                mm.then_inc(m_full, 1)
            pe.wait_ge(const_made, 4)
            pe.wait_ge(w_lo_done, W_PARTS)
            pe.wait_ge(out_w_loaded, 16 * N_OUT_W)

            def split_product(dst, w_hi, w_lo, v_hi, v_lo):
                pe.matmul(dst, w_hi, v_hi, start=True, stop=False)
                pe.matmul(dst, w_hi, v_lo, start=False, stop=False)
                return pe.matmul(dst, w_lo, v_hi, start=False, stop=True)

            def attn_waits(G):
                wait(pe, probsT_done, G - 1)
                wait(pe, value_done, G - 1)
                wait(pe, attnT_done, G - 2)
                wait(pe, res_done, G - 2)

            def window(T, prev, cur, nxt):
                for s in range(STEPS):
                    G = STEPS * T + s
                    item = ln_item(s, prev, cur, nxt)
                    if item:
                        k, i, off = item
                        n = PAIRS * (T + off) + i
                        wait(pe, z_done[k - 1], n + 1)
                        if i > 0:
                            wait(pe, h_done[k - 1], n)
                        elif k == 3:
                            wait(pe, h_done[1], PAIRS * T)
                            wait(pe, out_done, PAIRS * (T - 1))
                        elif k == 2 and nxt:
                            wait(pe, h_done[0], PAIRS * (T + 2))
                        else:
                            wait(pe, h_done[2], PAIRS * T)
                        pe.transpose(ln_ps[:, 0:P], z[:, i % 2, :], ident[:, :]).then_inc(turned[k - 1], 1)
                    lagged = cur if s >= 2 else prev
                    if lagged:
                        wait(pe, probs_done, G - 1)
                        wait(pe, probsT_done, G - 2)
                        for hp in range(HP):
                            mm = pe.transpose(turn_ps[:, hp, :], probs[:, (s - 2) % 4, hp, :], ident[:, :])
                        mm.then_inc(turn_full, 1)
                    j = G + PAIRS
                    projecting = cur if s < STEPS - PAIRS else nxt
                    nb = (s // PAIRS + 1) % BLOCKS
                    a, half = nb // 2, nb % 2
                    rows = cdim[a]
                    src_hi, src_lo = ((h1_hi, h1_lo), (c_hi, c_lo))[a]
                    if projecting:
                        if s == STEPS - PAIRS:
                            wait(pe, lo_done[0], PAIRS * (T + 2))
                        if s == PAIRS:
                            wait(pe, c_lo_done, T + 1)
                        for u in range(2):
                            head = half * HALF + 2 * (s % PAIRS) + u
                            wait(pe, key_done, 2 * j + u - 1)
                            if prev and FF_AT < s <= FF_AT + FFC:
                                wait(pe, (gate_done, up_done)[u], FFC * (T - 1) + s - FF_AT)
                            split_product(key_ps[u][:, :], m_hi[a][0:rows, head, :], m_lo[a][0:rows, head, :],
                                          src_hi[0:rows, :], src_lo[0:rows, :]).then_inc(key_full, 1)
                    if cur:
                        blk, i = s // PAIRS, s % PAIRS
                        if i == 0:
                            wait(pe, key_done, 2 * (G + PAIRS))
                        h = h1 if blk < 2 else h2
                        if blk == 2:
                            wait(pe, h_done[1], PAIRS * T + i + 1)
                        wait(pe, sub_done, G)
                        dst = scores_ps[:, :].rearrange("p (h b k) -> p h b k", b=2, k=SEQ)
                        by_head = keys[:, blk % 2, :, :].rearrange("p (h q) t -> p h q t", q=2)
                        for b in range(2):
                            cols = slice(i * P + b * SEQ, i * P + (b + 1) * SEQ)
                            for par in range(2):
                                if lagged and (b, par) == (1, 1):
                                    attn_waits(G)
                                mm = pe.matmul(dst[par * SEQ:(par + 1) * SEQ, :, b, :], h[:, cols],
                                               by_head[:, :, par, cols], start=True, stop=True)
                        mm.then_inc(scores_full, 1)
                    if lagged:
                        buf = (s - 2) % STEPS // PAIRS % 2
                        pair = (s - 2) % PAIRS
                        if not cur:
                            attn_waits(G)
                        for hp in range(HP):
                            for b, par in ((0, 0), (1, 1), (0, 1), (1, 0)):
                                keys_of = slice(b * SEQ, (b + 1) * SEQ)
                                h = 2 * hp + par
                                mm = pe.matmul(attn_ps[par * DH:(par + 1) * DH, b, hp * SEQ:(hp + 1) * SEQ],
                                               values[keys_of, buf, pair, h * DH:(h + 1) * DH],
                                               probsT[keys_of, s % 2, hp, par * SEQ:(par + 1) * SEQ],
                                               start=True, stop=True)
                        mm.then_inc(attn_full, 1)
                    if projecting:
                        tok = slice(s % PAIRS * P, (s % PAIRS + 1) * P)
                        cols = slice(half * HALF * DH, (half + 1) * HALF * DH)
                        wait(pe, value_done, j)
                        split_product(value_ps[:, :], src_hi[0:rows, tok], src_lo[0:rows, tok],
                                      wv_hi[a][0:rows, cols], wv_lo[a][0:rows, cols]).then_inc(value_full, 1)
                    if prev and FF_AT <= s < FF_AT + FFC:
                        i = s - FF_AT
                        if i == 0:
                            wait(pe, lo_done[2], PAIRS * T)
                        wait(pe, key_done, 2 * j + 2 if cur else 2 * STEPS * n_tiles)
                        wait(pe, gate_done, FFC * (T - 1) + i)
                        wait(pe, up_done, FFC * (T - 1) + i)
                        for ps, c, full in ((key_ps[0], FFC + i, gate_full), (key_ps[1], i, up_full)):
                            cols = slice(c * P, (c + 1) * P)
                            split_product(ps[:, :], wp_hi[:, cols], wp_lo[:, cols], h3_hi[:, :], h3_lo[:, :])\
                                .then_inc(full, 1)
                    if prev and DOWN_AT <= s < DOWN_AT + PAIRS:
                        i = s - DOWN_AT
                        if i == 0:
                            wait(pe, gated, FFC * T)
                            wait(pe, h_done[1], PAIRS * (T + 1) if cur else PAIRS * T)
                        wait(pe, out_done, PAIRS * (T - 1) + i)
                        for c in range(FFC):
                            mm = pe.matmul(down_ps, up[:, c, i * P:(i + 1) * P], w2_sb[:, c, :],
                                           start=(c == 0), stop=(c == FFC - 1))
                        mm.then_inc(down_full, 1)
                    if lagged:
                        blk = (s - 2) % STEPS // PAIRS
                        wait(pe, attnT_done, G - 1)
                        for hp in range(HP):
                            mm = pe.matmul(proj_ps, attnT[:, s % 2, hp, :, :].rearrange("p b q -> p (b q)"),
                                           wo_sb[blk // 2][:, blk % 2 * HP + hp, :],
                                           start=(hp == 0), stop=(hp == HP - 1))
                        mm.then_inc(proj_full, 1)

            windows(pe, window)


def kernel(x, ctx_768, L0_xattn_Wq1, L0_xattn_Wk1, L0_xattn_Wv1, L0_xattn_Wo1, L0_xattn_bo1, L0_xattn_Wq2,
           L0_xattn_Wk2, L0_xattn_Wv2, L0_xattn_Wo2, L0_xattn_bo2, L0_xattn_Wp, L0_xattn_bp, L0_xattn_W2,
           L0_xattn_b2, L0_xattn_g1, L0_xattn_be1, L0_xattn_g2, L0_xattn_be2, L0_xattn_g3, L0_xattn_be3):
    import numpy as np
    import concourse.bacc as bacc
    from concourse.bass_utils import run_bass_kernel_spmd

    x = np.asarray(x)
    n_tok = x.shape[0] * x.shape[1]

    def col(*vs):
        return np.stack([np.asarray(v) for v in vs], axis=1)

    arrays = {
        "x": x.reshape(n_tok, P),
        "ctxT": np.asarray(ctx_768).reshape(n_tok // TOK, TOK, CTX).transpose(0, 2, 1),
        "wq1T": np.asarray(L0_xattn_Wq1).T, "wq2T": np.asarray(L0_xattn_Wq2).T,
        "wk1T": np.asarray(L0_xattn_Wk1).T, "wk2T": np.asarray(L0_xattn_Wk2).T,
        "wv1": np.asarray(L0_xattn_Wv1), "wv2": np.asarray(L0_xattn_Wv2),
        "wo1": np.asarray(L0_xattn_Wo1), "wo2": np.asarray(L0_xattn_Wo2),
        "bo1": np.asarray(L0_xattn_bo1), "bo2": np.asarray(L0_xattn_bo2),
        "wp": np.asarray(L0_xattn_Wp), "bp": np.asarray(L0_xattn_bp).reshape(2 * FFC, P).T,
        "w2": np.asarray(L0_xattn_W2), "b2": np.asarray(L0_xattn_b2),
        "ln_g": col(L0_xattn_g1, L0_xattn_g2, L0_xattn_g3),
        "ln_b": col(L0_xattn_be1, L0_xattn_be2, L0_xattn_be3),
    }
    arrays = {f"in_{k}": np.ascontiguousarray(v) for k, v in arrays.items()}
    nc = bacc.Bacc("TRN2", target_bir_lowering=False, num_devices=1)
    d = {k[3:]: nc.dram_tensor(k, v.shape, mybir.dt.from_np(v.dtype), kind="ExternalInput").ap()
         for k, v in arrays.items()}
    out = nc.dram_tensor("out_y", (n_tok, P), F32, kind="ExternalOutput").ap()
    block_kernel(nc, d["x"], d["ctxT"], [d["wq1T"], d["wq2T"]], [d["wk1T"], d["wk2T"]], [d["wv1"], d["wv2"]],
                 [d["wo1"], d["wo2"]], [d["bo1"], d["bo2"]], d["wp"], d["bp"], d["w2"], d["b2"], d["ln_g"],
                 d["ln_b"], out)
    r = run_bass_kernel_spmd(nc, [arrays], core_ids=[0])
    return r.results[0]["out_y"].reshape(x.shape)
```

```python
from contextlib import ExitStack

import concourse.bass as bass
from concourse import mybir

ALU = mybir.AluOpType
ACT = mybir.ActivationFunctionType
F32 = mybir.dt.float32
F32R = mybir.dt.float32r
AX_X = mybir.AxisListType.X

P = 128
SEQ = 64
DH = 64
HEADS = 16
CTX = 96
FF = 512
EPS = 1e-5
SCALE = DH ** -0.5

TOK = 512
PAIRS = TOK // P
HALF = HEADS // 2
HP = HALF // 2
STEPS = 2 * 2 * PAIRS
BLOCKS = STEPS // PAIRS
FFC = FF // P
LN1_AT, LN2_AT, LN3_AT = PAIRS, 2 * PAIRS, 0
FF_AT = PAIRS
GELU_AT = FF_AT + FFC
TURN_BY_DVE = GELU_AT + 1
DOWN_AT = 11


def wait(eng, sem, value):
    if not (isinstance(value, int) and value <= 0):
        eng.wait_ge(sem, value)


def f32(ap):
    return ap.bitcast(F32)


def block_kernel(nc, x, ctxT, wqT, wkT, wv, wo, bo, wp, bp, w2, b2, ln_g, ln_b, out):
    n_tiles = x.shape[0] // TOK
    assert ctxT.shape == (n_tiles, CTX, TOK) and n_tiles >= 4

    with ExitStack() as stack:
        def sb(name, shape, dt=F32):
            return stack.enter_context(nc.sbuf_tensor(name, shape, dt))

        def pb(name, shape):
            return stack.enter_context(nc.psum_tensor(name, shape, F32))

        def sem(name):
            return stack.enter_context(nc.semaphore(name))

        m_hi = [sb(f"m{a}_hi", [P, HEADS, P], F32R) for a in (1, 2)]
        m_lo = [sb(f"m{a}_lo", [P, HEADS, P], F32R) for a in (1, 2)]
        wv_hi = [sb(f"wv{a}_hi", [P, HEADS * DH], F32R) for a in (1, 2)]
        wv_lo = [sb(f"wv{a}_lo", [P, HEADS * DH], F32R) for a in (1, 2)]
        wo_sb = [sb(f"wo{a}_sb", [P, HEADS // 2, P]) for a in (1, 2)]
        wp_hi = sb("wp_hi", [P, 2 * FF], F32R)
        wp_lo = sb("wp_lo", [P, 2 * FF], F32R)
        w2_sb = sb("w2_sb", [P, FFC, P])
        bo_sb = [sb(f"bo{a}_sb", [P, P]) for a in (1, 2)]
        b2_sb = sb("b2_sb", [P, P])
        bp_sb = sb("bp_sb", [P, 2 * FFC])
        g_sb = sb("g_sb", [P, 3])
        be_sb = sb("be_sb", [P, 3])
        ident = sb("ident", [P, P])
        minus_half = sb("minus_half", [P, 1])
        eps_sb = sb("eps_sb", [P, 1])

        x_in = sb("x_in", [P, PAIRS, P])
        x_bo1 = sb("x_bo1", [P, PAIRS, P])
        x1 = sb("x1", [P, PAIRS, P])
        x1_bo2 = sb("x1_bo2", [P, PAIRS, P])
        x2 = sb("x2", [P, PAIRS, P])
        x2_b2 = sb("x2_b2", [P, PAIRS, P])
        y_out = sb("y_out", [P, PAIRS, P])
        z = sb("z", [P, 2, P])
        stats = sb("stats", [P, 6])
        mean_var = [sb(f"mean_var{k}", [P, 2, 2]) for k in (1, 2, 3)]
        var_eps = [sb(f"var_eps{k}", [P, 2]) for k in (1, 2, 3)]
        rstd = [sb(f"rstd{k}", [P, 2]) for k in (1, 2, 3)]

        h1, h2, h3 = (sb(f"h{k}", [P, TOK]) for k in (1, 2, 3))
        h1_hi, h1_lo = sb("h1_hi", [P, TOK], F32R), sb("h1_lo", [P, TOK], F32R)
        h3_hi, h3_lo = sb("h3_hi", [P, TOK], F32R), sb("h3_lo", [P, TOK], F32R)
        c_in = sb("c_in", [P, TOK])
        c_hi, c_lo = sb("c_hi", [P, TOK], F32R), sb("c_lo", [P, TOK], F32R)
        gate = sb("gate", [P, FFC, TOK])
        up = sb("up", [P, FFC, TOK])

        keys = sb("keys", [P, 2, HALF, TOK])
        values = sb("values", [P, 2, PAIRS, HALF * DH])
        probs = sb("probs", [P, 4, HP, P])
        probsT = sb("probsT", [P, 2, HP, P])
        attnT = sb("attnT", [P, 2, HP, 2, SEQ])
        row_max = sb("row_max", [P, 2, 2 * HP])
        row_sum = sb("row_sum", [P, 2, 2 * HP])
        row_inv = sb("row_inv", [P, 2, 2 * HP])

        scores_ps = pb("scores_ps", [P, 512])
        turn_ps = pb("turn_ps", [P, HP, P])
        attn_ps = pb("attn_ps", [P, 2, 512])
        key_ps = [pb(f"key_ps{i}", [P, 512]) for i in range(2)]
        value_ps = pb("value_ps", [P, 512])
        ln_ps = pb("ln_ps", [P, 512])
        proj_ps = attn_ps[:, 0, 256:384]
        down_ps = ln_ps[:, 256:384]

        W = HEADS * DH
        raw = [keys[:, a, :, :].rearrange("p h t -> p (h t)") for a in (0, 1)]
        wqT_raw = [r[:, 0:W].rearrange("p (c n) -> p c n", n=P) for r in raw]
        cdim = [P, CTX]
        wkT_raw = [r[:, W:W + HEADS // 2 * n].rearrange("p (c n) -> p c n", n=n) for r, n in zip(raw, cdim)]
        wv_raw = [r[:, 2 * W:3 * W] for r in raw]
        wp_raw = raw[1][:, 3 * W:4 * W]
        banks = [scores_ps[:, :], turn_ps[:, :, :].rearrange("p a b -> p (a b)"), attn_ps[:, 0, :],
                 attn_ps[:, 1, :]]

        qk_loaded = [sem(f"qk_loaded{a}") for a in (1, 2)]
        v_loaded = [sem(f"v_loaded{a}") for a in (1, 2)]
        p_loaded = sem("p_loaded")
        small_loaded = sem("small_loaded")
        out_w_loaded = sem("out_w_loaded")
        const_made = sem("const_made")
        m_full = sem("m_full")
        w_hi_done = sem("w_hi_done")
        w_lo_done = sem("w_lo_done")
        x_loaded = sem("x_loaded")
        ctx_loaded = sem("ctx_loaded")
        stored = sem("stored")
        stat_done = [sem(f"stat_done{k}") for k in (1, 2, 3)]
        raw_stat = sem("raw_stat")
        eps_added = sem("eps_added")
        rstd_done = [sem(f"rstd_done{k}") for k in (1, 2, 3)]
        z_done = [sem(f"z_done{k}") for k in (1, 2, 3)]
        turned = [sem(f"ln_turned{k}") for k in (1, 2, 3)]
        h_done = [sem(f"h_done{k}") for k in (1, 2, 3)]
        hi_done = [sem(f"hi_done{k}") for k in (1, 2, 3)]
        lo_done = [sem(f"lo_done{k}") for k in (1, 2, 3)]
        c_hi_done = sem("c_hi_done")
        c_lo_done = sem("c_lo_done")
        key_full = sem("key_full")
        key_done = sem("key_done")
        value_full = sem("value_full")
        value_done = sem("value_done")
        scores_full = sem("scores_full")
        max_done = sem("max_done")
        sub_done = sem("sub_done")
        exp_done = sem("exp_done")
        sum_done = sem("sum_done")
        inv_done = sem("inv_done")
        probs_done = sem("probs_done")
        turn_full = sem("turn_full")
        probsT_done = sem("probsT_done")
        attn_full = sem("attn_full")
        attnT_done = sem("attnT_done")
        proj_full = sem("proj_full")
        res_done = sem("res_done")
        x_bo1_done = sem("x_bo1_done")
        x1_bo2_done = sem("x1_bo2_done")
        x2_b2_done = sem("x2_b2_done")
        gate_full = sem("gate_full")
        gate_done = sem("gate_done")
        up_full = sem("up_full")
        up_done = sem("up_done")
        gelu_done = sem("gelu_done")
        gated = sem("gated")
        down_full = sem("down_full")
        out_done = sem("out_done")

        SMALL, OUT_W = 16 * 6, 16 * 3
        PARTS1, PARTS = 5, 11

        def windows(eng, window):
            window(0, False, True, True)
            window(1, True, True, True)
            with eng.Fori(2, n_tiles - 1) as T:
                window(T, True, True, True)
            window(n_tiles - 1, True, True, False)
            window(n_tiles, True, False, False)

        FIRST_LN, FIRST_PROJ = range(LN1_AT - 1, LN1_AT + PAIRS + 1), range(STEPS - PAIRS, STEPS)

        def ln_item(s, prev, cur, nxt):
            for k, at, off, on in ((1, LN1_AT, 1, nxt), (2, LN2_AT, 0, cur), (3, LN3_AT, -1, prev)):
                if on and at <= s < at + PAIRS:
                    return k, s - at, off
            return None

        def ln_item_next(s, prev, cur, nxt):
            if s == STEPS - 1:
                return (3, 0, 0) if cur else None
            return ln_item(s + 1, prev, cur, nxt)

        def eps_count(T, s, prev, cur, nxt):
            in_window = sum(ln_item_next(q, prev, cur, nxt) is not None for q in range(s + 1))
            if isinstance(T, int):
                before = {-1: 0, 0: PAIRS}.get(T, PAIRS + (2 * PAIRS + 1) + 3 * PAIRS * (T - 1))
                if T == n_tiles:
                    before -= PAIRS
            else:
                before = PAIRS + (2 * PAIRS + 1) - 3 * PAIRS + 3 * PAIRS * T
            return before + in_window

        block = stack.enter_context(nc.Block())

        @block.sync
        def _(sp):
            def load_x(t):
                wait(sp, z_done[0], PAIRS * t)
                wait(sp, x_bo1_done, PAIRS * t)
                sp.dma_start(x_in[:, :, :], x[bass.ts(t, TOK), :].rearrange("(c p) d -> p c d", p=P))\
                    .then_inc(x_loaded, 16)

            def load_ctx(t):
                wait(sp, c_lo_done, t)
                sp.dma_start(c_in[0:CTX, :], ctxT[bass.ts(t, 1), :, :].rearrange("a c t -> c (a t)"))\
                    .then_inc(ctx_loaded, 16)

            def store(t):
                sp.wait_ge(out_done, PAIRS * t + PAIRS)
                sp.dma_start(out[bass.ts(t, TOK), :].rearrange("(c p) d -> p c d", p=P), y_out[:, :, :])\
                    .then_inc(stored, 16)

            load_x(0)
            for a in range(2):
                sp.dma_start(wqT_raw[a], wqT[a].rearrange("(c p) n -> p c n", p=P)).then_inc(qk_loaded[a], 16)
                sp.dma_start(wkT_raw[a], wkT[a].rearrange("(c p) n -> p c n", p=P)).then_inc(qk_loaded[a], 16)
                sp.dma_start(wv_raw[a][0:cdim[a], :], wv[a]).then_inc(v_loaded[a], 16)
            sp.dma_start(wp_raw, wp).then_inc(p_loaded, 16)
            load_ctx(0)
            load_x(1)
            load_ctx(1)
            with sp.Fori(2, n_tiles) as t:
                load_x(t)
                load_ctx(t)
                store(t - 2)
            for t in (n_tiles - 2, n_tiles - 1):
                store(t)
            sp.wait_ge(stored, 16 * n_tiles)

        @block.gpsimd
        def _(pool):
            pool.memset(minus_half[:, :], -0.5).then_inc(const_made, 1)
            pool.memset(ident[:, :], 0.0).then_inc(const_made, 1)
            pool.memset(eps_sb[:, :], EPS).then_inc(const_made, 1)
            pool.wait_ge(const_made, 3)
            pool.affine_select(out=ident[:, :], in_=ident[:, :], compare_op=ALU.not_equal, fill=1.0, base=0,
                               pattern=[[-1, P]], channel_multiplier=1).then_inc(const_made, 1)
            pool.wait_ge(const_made, 4)
            pool.wait_ge(small_loaded, SMALL)

            def window(T, prev, cur, nxt, steps=range(STEPS)):
                for s in steps:
                    G = STEPS * T + s
                    if item := ln_item_next(s, prev, cur, nxt):
                        k, i, off = item
                        n = PAIRS * (T + off) + i
                        wait(pool, stat_done[k - 1], n + 1)
                        slot = i % 2
                        pool.tensor_tensor(var_eps[k - 1][:, slot:slot + 1], mean_var[k - 1][:, slot, 1:2],
                                           eps_sb[:, :], ALU.add).then_inc(eps_added, 1)
                        wait(pool, eps_added, eps_count(T, s, prev, cur, nxt))
                        pool.tensor_tensor(rstd[k - 1][:, slot:slot + 1], var_eps[k - 1][:, slot:slot + 1],
                                           minus_half[:, :], ALU.pow).then_inc(rstd_done[k - 1], 1)
                    if prev and s < PAIRS:
                        n = PAIRS * (T - 1) + s
                        cols = slice(s * P, (s + 1) * P)
                        wait(pool, hi_done[2], n + 1)
                        pool.tensor_tensor(h3_lo[:, cols], h3[:, cols], f32(h3_hi[:, cols]), ALU.subtract)\
                            .then_inc(lo_done[2], 1)
                        wait(pool, res_done, STEPS * (T - 1) + 3 * PAIRS + s + 1)
                        pool.tensor_tensor(x2_b2[:, s, :], x2[:, s, :], b2_sb[:, :], ALU.add)\
                            .then_inc(x2_b2_done, 1)
                    if nxt and LN1_AT <= s < LN1_AT + PAIRS:
                        i = s - LN1_AT
                        wait(pool, x_loaded, 16 * (T + 2))
                        wait(pool, res_done, STEPS * T + i + 1)
                        pool.tensor_tensor(x_bo1[:, i, :], x_in[:, i, :], bo_sb[0][:, :], ALU.add)\
                            .then_inc(x_bo1_done, 1)
                    if nxt and LN1_AT < s <= LN1_AT + PAIRS:
                        i = s - LN1_AT - 1
                        cols = slice(i * P, (i + 1) * P)
                        wait(pool, hi_done[0], PAIRS * (T + 1) + i + 1)
                        pool.tensor_tensor(h1_lo[:, cols], h1[:, cols], f32(h1_hi[:, cols]), ALU.subtract)\
                            .then_inc(lo_done[0], 1)
                    if cur and s == 2:
                        wait(pool, c_hi_done, T + 1)
                        pool.tensor_tensor(c_lo[0:CTX, :], c_in[0:CTX, :], f32(c_hi[0:CTX, :]), ALU.subtract)\
                            .then_inc(c_lo_done, 1)
                    if cur and LN2_AT <= s < LN2_AT + PAIRS:
                        i = s - LN2_AT
                        wait(pool, res_done, STEPS * T + PAIRS + i + 1)
                        pool.tensor_tensor(x1_bo2[:, i, :], x1[:, i, :], bo_sb[1][:, :], ALU.add)\
                            .then_inc(x1_bo2_done, 1)
                    if prev and cur and GELU_AT < s <= GELU_AT + 2:
                        wait(pool, gelu_done, T)
                        wait(pool, up_done, FFC * T)
                        for j in range(2 * (s - GELU_AT - 1), 2 * (s - GELU_AT)):
                            pool.tensor_tensor(up[:, j, :], up[:, j, :], gate[:, j, :], ALU.mult)\
                                .then_inc(gated, 1)

            window(-1, False, False, True, FIRST_LN)
            windows(pool, window)

        @block.scalar
        def _(act):
            act.dma_start(g_sb[:, :], ln_g).then_inc(small_loaded, 16)
            act.dma_start(be_sb[:, :], ln_b).then_inc(small_loaded, 16)
            act.dma_start(bp_sb[:, :], bp).then_inc(small_loaded, 16)
            for dst, src in ((bo_sb[0], bo[0]), (bo_sb[1], bo[1]), (b2_sb, b2)):
                act.dma_start(dst[:, :], src.partition_broadcast(P)).then_inc(small_loaded, 16)
            for a in range(2):
                act.dma_start(wo_sb[a][:, :, :], wo[a].rearrange("(c p) n -> p c n", p=P))\
                    .then_inc(out_w_loaded, 16)
            act.dma_start(w2_sb[:, :, :], w2.rearrange("(c p) n -> p c n", p=P)).then_inc(out_w_loaded, 16)

            def split_weights(a):
                heads = m_hi[a][0:cdim[a], :, :].rearrange("p (c q) n -> p c q n", q=2)
                for n in range(4):
                    par, c = n // 2, n % 2
                    act.wait_ge(m_full, 4 * a + n + 1)
                    act.activation(heads[:, 4 * c:4 * c + 4, par, :],
                                   banks[n][0:cdim[a], :].rearrange("p (c n) -> p c n", n=P),
                                   ACT.Copy, scale=SCALE).then_inc(w_hi_done, 1)
                act.wait_ge(v_loaded[a], 16)
                act.activation(wv_hi[a][0:cdim[a], :], wv_raw[a][0:cdim[a], :], ACT.Copy).then_inc(w_hi_done, 1)

            def window(T, prev, cur, nxt, steps=range(STEPS)):
                for s in steps:
                    G = STEPS * T + s
                    lagged = cur if s >= 2 else prev
                    if lagged and s != TURN_BY_DVE:
                        wait(act, turn_full, G - 1)
                        wait(act, attn_full, G - 3)
                        act.activation(probsT[:, s % 2, :, :], turn_ps[:, :, :], ACT.Copy)\
                            .then_inc(probsT_done, 1)
                    j = G + PAIRS
                    projecting = cur if s < STEPS - PAIRS else nxt
                    buf = (s // PAIRS + 1) % 2

                    def key_copy(u):
                        wait(act, key_full, 2 * j + u + 1)
                        act.activation(keys[:, buf, 2 * (s % PAIRS) + u, :], key_ps[u][:, :], ACT.Copy)\
                            .then_inc(key_done, 1)

                    if projecting:
                        if s % PAIRS == 0:
                            wait(act, scores_full, j - PAIRS)
                        key_copy(0)
                    if prev and s < PAIRS:
                        cols = slice(s * P, (s + 1) * P)
                        wait(act, h_done[2], PAIRS * (T - 1) + s + 1)
                        act.activation(h3_hi[:, cols], h3[:, cols], ACT.Copy).then_inc(hi_done[2], 1)
                    if nxt and LN1_AT < s <= LN1_AT + PAIRS:
                        i = s - LN1_AT - 1
                        cols = slice(i * P, (i + 1) * P)
                        wait(act, h_done[0], PAIRS * (T + 1) + i + 1)
                        act.activation(h1_hi[:, cols], h1[:, cols], ACT.Copy).then_inc(hi_done[0], 1)
                    if lagged:
                        wait(act, attn_full, G - 1)
                        wait(act, proj_full, G - 3)
                        act.activation(attnT[:, s % 2, :, :, :].rearrange("p h b q -> p b h q"),
                                       attn_ps[:, :, 0:HP * SEQ].rearrange("p b (h q) -> p b h q", q=SEQ),
                                       ACT.Copy).then_inc(attnT_done, 1)
                    if projecting:
                        key_copy(1)
                        wait(act, value_full, j + 1)
                        wait(act, attn_full, j - 2 * PAIRS + 1)
                        act.activation(values[:, buf, s % PAIRS, :], value_ps[:, :], ACT.Copy)\
                            .then_inc(value_done, 1)
                    if cur:
                        wait(act, sub_done, G + 1)
                        e = probs[:, s % 4, :, :]
                        act.activation(e, e, ACT.Exp).then_inc(exp_done, 1)
                    if cur and s == 1:
                        wait(act, ctx_loaded, 16 * (T + 1))
                        act.activation(c_hi[0:CTX, :], c_in[0:CTX, :], ACT.Copy).then_inc(c_hi_done, 1)
                    if prev and FF_AT <= s < FF_AT + FFC:
                        i = s - FF_AT
                        wait(act, gate_full, FFC * (T - 1) + i + 1)
                        wait(act, gated, FFC * (T - 1))
                        act.activation(gate[:, i, :], key_ps[0][:, :], ACT.Identity if cur else ACT.Gelu,
                                       bias=bp_sb[:, FFC + i:FFC + i + 1]).then_inc(gate_done, 1)
                    if prev and cur and s == GELU_AT:
                        wait(act, gate_done, FFC * T)
                        act.activation(gate[:, :, :], gate[:, :, :], ACT.Gelu).then_inc(gelu_done, 1)

            act.wait_ge(small_loaded, SMALL)
            window(-1, False, False, True, FIRST_LN)
            split_weights(0)
            window(-1, False, False, True, FIRST_PROJ)
            split_weights(1)
            act.wait_ge(p_loaded, 16)
            act.activation(wp_hi[:, :], wp_raw, ACT.Copy).then_inc(w_hi_done, 1)
            windows(act, window)

        @block.vector
        def _(dve):
            def low_part(n, dst, src, hi, rows):
                dve.wait_ge(w_hi_done, n)
                dve.tensor_tensor(dst[0:rows, :], src[0:rows, :], f32(hi[0:rows, :]), ALU.subtract)\
                    .then_inc(w_lo_done, 1)

            def split_weights(a):
                hi = f32(m_hi[a][0:cdim[a], :, :]).rearrange("p (c q) n -> p c q n", q=2)
                lo = m_lo[a][0:cdim[a], :, :].rearrange("p (c q) n -> p c q n", q=2)
                for n in range(4):
                    par, c = n // 2, n % 2
                    dve.wait_ge(w_hi_done, PARTS1 * a + n + 1)
                    dve.scalar_tensor_tensor(out=lo[:, 4 * c:4 * c + 4, par, :],
                                             in0=banks[n][0:cdim[a], :].rearrange("p (c n) -> p c n", n=P),
                                             scalar=SCALE, in1=hi[:, 4 * c:4 * c + 4, par, :],
                                             op0=ALU.mult, op1=ALU.subtract).then_inc(w_lo_done, 1)
                low_part(PARTS1 * (a + 1), wv_lo[a], wv_raw[a], wv_hi[a], cdim[a])

            def ln_out(k, i, off, T, h):
                wait(dve, turned[k - 1], PAIRS * (T + off) + i + 1)
                dve.tensor_scalar(h[:, i * P:(i + 1) * P], ln_ps[:, 0:P], g_sb[:, k - 1:k], be_sb[:, k - 1:k],
                                  ALU.mult, ALU.add).then_inc(h_done[k - 1], 1)

            def window(T, prev, cur, nxt, steps=range(STEPS)):
                for s in steps:
                    G = STEPS * T + s
                    if cur if s >= 3 else prev:
                        q = (s - 3) % STEPS
                        t = T if s >= 3 else T - 1
                        i = q % PAIRS
                        wait(dve, proj_full, G - 2)
                        if q // PAIRS == 0:
                            wait(dve, x_bo1_done, PAIRS * t + i + 1)
                            wait(dve, x1_bo2_done, PAIRS * (t - 1) + i + 1)
                            dst, src = x1[:, i, :], x_bo1[:, i, :]
                        elif q // PAIRS == 1:
                            dst, src = x1[:, i, :], x1[:, i, :]
                        elif q // PAIRS == 2:
                            wait(dve, x1_bo2_done, PAIRS * t + i + 1)
                            wait(dve, x2_b2_done, PAIRS * (t - 1) + i + 1)
                            dst, src = x2[:, i, :], x1_bo2[:, i, :]
                        else:
                            dst, src = x2[:, i, :], x2[:, i, :]
                        if q // PAIRS % 2:
                            wait(dve, res_done, G - 3 - PAIRS + 1)
                        dve.tensor_tensor(dst, proj_ps, src, ALU.add).then_inc(res_done, 1)
                    if prev and DOWN_AT < s <= DOWN_AT + PAIRS:
                        i = s - DOWN_AT - 1
                        wait(dve, down_full, PAIRS * (T - 1) + i + 1)
                        wait(dve, x2_b2_done, PAIRS * (T - 1) + i + 1)
                        if i == 0:
                            wait(dve, stored, 16 * (T - 1))
                        dve.tensor_tensor(y_out[:, i, :], down_ps, x2_b2[:, i, :], ALU.add).then_inc(out_done, 1)
                    item = ln_item(s, prev, cur, nxt)
                    if item and item[0] != 1:
                        ln_out(*item, T, h2 if item[0] == 2 else h3)
                    after = ln_item_next(s, prev, cur, nxt)
                    if after:
                        k, i, off = after
                        n = PAIRS * (T + off) + i
                        src = (x_in, x1, x2)[k - 1][:, i, :]
                        if k == 1:
                            wait(dve, x_loaded, 16 * (T + 2))
                        else:
                            wait(dve, res_done, G - 2)
                        dve.bn_stats(stats[:, :], src).then_inc(raw_stat, 1)
                    if cur and s == TURN_BY_DVE:
                        wait(dve, turn_full, G - 1)
                        wait(dve, attn_full, G - 3)
                        dve.tensor_copy(probsT[:, s % 2, :, :], turn_ps[:, :, :]).then_inc(probsT_done, 1)
                    if cur if s >= 1 else prev:
                        e = probs[:, (s - 1) % 4, :, :].rearrange("p h (b k) -> p (h b) k", k=SEQ)
                        r = (s - 1) % 2
                        wait(dve, exp_done, G)
                        if after:
                            wait(dve, raw_stat, eps_count(T, s, prev, cur, nxt))
                        dve.tensor_reduce(row_sum[:, r, :], e, AX_X, ALU.add).then_inc(sum_done, 1)
                    elif after:
                        wait(dve, raw_stat, eps_count(T, s, prev, cur, nxt))
                    if after:
                        dve.bn_aggr(mean_var[k - 1][:, i % 2, :], stats[:, :]).then_inc(stat_done[k - 1], 1)
                    if cur if s >= 1 else prev:
                        wait(dve, sum_done, G)
                        dve.reciprocal(row_inv[:, r, :], row_sum[:, r, :]).then_inc(inv_done, 1)
                        wait(dve, inv_done, G)
                        dve.tensor_tensor(e, e, row_inv[:, r, :].unsqueeze(2).to_broadcast([P, 2 * HP, SEQ]),
                                          ALU.mult).then_inc(probs_done, 1)
                    if after:
                        wait(dve, rstd_done[k - 1], n + 1)
                        if i >= 2:
                            wait(dve, turned[k - 1], n - 1)
                        dve.tensor_scalar(z[:, i % 2, :], src, mean_var[k - 1][:, i % 2, 0:1],
                                          rstd[k - 1][:, i % 2:i % 2 + 1], ALU.subtract, ALU.mult)\
                            .then_inc(z_done[k - 1], 1)
                    if cur:
                        sc = scores_ps[:, :].rearrange("p (g k) -> p g k", k=SEQ)
                        e = probs[:, s % 4, :, :].rearrange("p h (b k) -> p (h b) k", k=SEQ)
                        r = s % 2
                        wait(dve, scores_full, G + 1)
                        dve.tensor_reduce(row_max[:, r, :], sc, AX_X, ALU.max).then_inc(max_done, 1)
                        wait(dve, max_done, G + 1)
                        wait(dve, turn_full, G - 3)
                        dve.tensor_tensor(e, sc, row_max[:, r, :].unsqueeze(2).to_broadcast([P, 2 * HP, SEQ]),
                                          ALU.subtract).then_inc(sub_done, 1)
                    if item and item[0] == 1:
                        ln_out(*item, T, h1)
                    if prev and FF_AT <= s < FF_AT + FFC:
                        i = s - FF_AT
                        wait(dve, up_full, FFC * (T - 1) + i + 1)
                        if cur:
                            dve.tensor_scalar(up[:, i, :], key_ps[1][:, :], bp_sb[:, i:i + 1], None, ALU.add)\
                                .then_inc(up_done, 1)
                        else:
                            wait(dve, gate_done, FFC * (T - 1) + i + 1)
                            dve.scalar_tensor_tensor(out=up[:, i, :], in0=key_ps[1][:, :],
                                                     scalar=bp_sb[:, i:i + 1], in1=gate[:, i, :], op0=ALU.add,
                                                     op1=ALU.mult).then_inc(up_done, 1)

            dve.wait_ge(small_loaded, SMALL)
            window(-1, False, False, True, FIRST_LN)
            split_weights(0)
            split_weights(1)
            low_part(PARTS, wp_lo, wp_raw, wp_hi, P)
            windows(dve, window)

        @block.tensor
        def _(pe):
            def build_m(a):
                pe.wait_ge(qk_loaded[a], 32)
                for n in range(4):
                    par, c = n // 2, n % 2
                    rows = slice(par * DH, (par + 1) * DH)
                    if a == 1:
                        pe.wait_ge(w_lo_done, n + 1)
                    for q in range(4):
                        mm = pe.matmul(banks[n][0:cdim[a], q * P:(q + 1) * P], wkT_raw[a][rows, 4 * c + q, :],
                                       wqT_raw[a][rows, 4 * c + q, :], start=True, stop=True)
                    mm.then_inc(m_full, 1)

            def split_product(dst, w_hi, w_lo, v_hi, v_lo):
                pe.matmul(dst, w_hi, v_hi, start=True, stop=False)
                pe.matmul(dst, w_hi, v_lo, start=False, stop=False)
                return pe.matmul(dst, w_lo, v_hi, start=False, stop=True)

            def attn_waits(G):
                wait(pe, probsT_done, G - 1)
                wait(pe, value_done, G - 1)
                wait(pe, attnT_done, G - 2)
                wait(pe, res_done, G - 2)

            def window(T, prev, cur, nxt, steps=range(STEPS)):
                for s in steps:
                    G = STEPS * T + s
                    item = ln_item(s, prev, cur, nxt)
                    if item:
                        k, i, off = item
                        n = PAIRS * (T + off) + i
                        wait(pe, z_done[k - 1], n + 1)
                        if i > 0:
                            wait(pe, h_done[k - 1], n)
                        elif k == 3:
                            wait(pe, h_done[1], PAIRS * T)
                            wait(pe, out_done, PAIRS * (T - 1))
                        elif k == 2 and nxt:
                            wait(pe, h_done[0], PAIRS * (T + 2))
                        else:
                            wait(pe, h_done[2], PAIRS * T)
                        pe.transpose(ln_ps[:, 0:P], z[:, i % 2, :], ident[:, :]).then_inc(turned[k - 1], 1)
                    lagged = cur if s >= 2 else prev
                    if lagged:
                        wait(pe, probs_done, G - 1)
                        wait(pe, probsT_done, G - 2)
                        for hp in range(HP):
                            mm = pe.transpose(turn_ps[:, hp, :], probs[:, (s - 2) % 4, hp, :], ident[:, :])
                        mm.then_inc(turn_full, 1)
                    j = G + PAIRS
                    projecting = cur if s < STEPS - PAIRS else nxt
                    nb = (s // PAIRS + 1) % BLOCKS
                    a, half = nb // 2, nb % 2
                    rows = cdim[a]
                    src_hi, src_lo = ((h1_hi, h1_lo), (c_hi, c_lo))[a]

                    def key_unit(u):
                        head = half * HALF + 2 * (s % PAIRS) + u
                        wait(pe, key_done, 2 * j + u - 1)
                        if prev and FF_AT < s <= FF_AT + FFC:
                            wait(pe, (gate_done, up_done)[u], FFC * (T - 1) + s - FF_AT)
                        split_product(key_ps[u][:, :], m_hi[a][0:rows, head, :], m_lo[a][0:rows, head, :],
                                      src_hi[0:rows, :], src_lo[0:rows, :]).then_inc(key_full, 1)

                    if projecting:
                        if s == STEPS - PAIRS:
                            wait(pe, lo_done[0], PAIRS * (T + 2))
                        if s == PAIRS:
                            wait(pe, c_lo_done, T + 1)
                        key_unit(0)
                    if cur:
                        blk, i = s // PAIRS, s % PAIRS
                        if i == 0:
                            wait(pe, key_done, 2 * (G + PAIRS))
                        h = h1 if blk < 2 else h2
                        if blk == 2:
                            wait(pe, h_done[1], PAIRS * T + i + 1)
                        wait(pe, sub_done, G)
                        dst = scores_ps[:, :].rearrange("p (h b k) -> p h b k", b=2, k=SEQ)
                        by_head = keys[:, blk % 2, :, :].rearrange("p (h q) t -> p h q t", q=2)
                        for b in range(2):
                            cols = slice(i * P + b * SEQ, i * P + (b + 1) * SEQ)
                            for par in range(2):
                                if lagged and (b, par) == (1, 1):
                                    attn_waits(G)
                                mm = pe.matmul(dst[par * SEQ:(par + 1) * SEQ, :, b, :], h[:, cols],
                                               by_head[:, :, par, cols], start=True, stop=True)
                        mm.then_inc(scores_full, 1)
                    if lagged:
                        buf = (s - 2) % STEPS // PAIRS % 2
                        pair = (s - 2) % PAIRS
                        if not cur:
                            attn_waits(G)
                        for hp in range(HP):
                            for b, par in ((0, 0), (1, 1), (1, 0), (0, 1)):
                                keys_of = slice(b * SEQ, (b + 1) * SEQ)
                                h = 2 * hp + par
                                mm = pe.matmul(attn_ps[par * DH:(par + 1) * DH, b, hp * SEQ:(hp + 1) * SEQ],
                                               values[keys_of, buf, pair, h * DH:(h + 1) * DH],
                                               probsT[keys_of, s % 2, hp, par * SEQ:(par + 1) * SEQ],
                                               start=True, stop=True)
                        mm.then_inc(attn_full, 1)
                    if projecting:
                        key_unit(1)
                        tok = slice(s % PAIRS * P, (s % PAIRS + 1) * P)
                        cols = slice(half * HALF * DH, (half + 1) * HALF * DH)
                        wait(pe, value_done, j)
                        split_product(value_ps[:, :], src_hi[0:rows, tok], src_lo[0:rows, tok],
                                      wv_hi[a][0:rows, cols], wv_lo[a][0:rows, cols]).then_inc(value_full, 1)
                    if prev and FF_AT <= s < FF_AT + FFC:
                        i = s - FF_AT
                        if i == 0:
                            wait(pe, lo_done[2], PAIRS * T)
                        for u, c, full, done in ((0, FFC + i, gate_full, gate_done), (1, i, up_full, up_done)):
                            wait(pe, key_done, 2 * j + u + 1 if cur else 2 * STEPS * n_tiles)
                            wait(pe, done, FFC * (T - 1) + i)
                            ps = key_ps[u]
                            cols = slice(c * P, (c + 1) * P)
                            split_product(ps[:, :], wp_hi[:, cols], wp_lo[:, cols], h3_hi[:, :], h3_lo[:, :])\
                                .then_inc(full, 1)
                    if prev and DOWN_AT <= s < DOWN_AT + PAIRS:
                        i = s - DOWN_AT
                        if i == 0:
                            wait(pe, *((gated, FFC * T) if cur else (up_done, FFC * T)))
                            wait(pe, h_done[1], PAIRS * (T + 1) if cur else PAIRS * T)
                        wait(pe, out_done, PAIRS * (T - 1) + i)
                        for c in range(FFC):
                            mm = pe.matmul(down_ps, up[:, c, i * P:(i + 1) * P], w2_sb[:, c, :],
                                           start=(c == 0), stop=(c == FFC - 1))
                        mm.then_inc(down_full, 1)
                    if lagged:
                        blk = (s - 2) % STEPS // PAIRS
                        wait(pe, attnT_done, G - 1)
                        for hp in range(HP):
                            mm = pe.matmul(proj_ps, attnT[:, s % 2, hp, :, :].rearrange("p b q -> p (b q)"),
                                           wo_sb[blk // 2][:, blk % 2 * HP + hp, :],
                                           start=(hp == 0), stop=(hp == HP - 1))
                        mm.then_inc(proj_full, 1)

            pe.wait_ge(const_made, 4)
            window(-1, False, False, True, FIRST_LN)
            build_m(0)
            pe.wait_ge(w_lo_done, PARTS1)
            window(-1, False, False, True, FIRST_PROJ)
            build_m(1)
            pe.wait_ge(w_lo_done, PARTS)
            pe.wait_ge(out_w_loaded, OUT_W)
            windows(pe, window)


def kernel(x, ctx_768, L0_xattn_Wq1, L0_xattn_Wk1, L0_xattn_Wv1, L0_xattn_Wo1, L0_xattn_bo1, L0_xattn_Wq2,
           L0_xattn_Wk2, L0_xattn_Wv2, L0_xattn_Wo2, L0_xattn_bo2, L0_xattn_Wp, L0_xattn_bp, L0_xattn_W2,
           L0_xattn_b2, L0_xattn_g1, L0_xattn_be1, L0_xattn_g2, L0_xattn_be2, L0_xattn_g3, L0_xattn_be3):
    import numpy as np
    import concourse.bacc as bacc
    from concourse.bass_utils import run_bass_kernel_spmd

    x = np.asarray(x)
    n_tok = x.shape[0] * x.shape[1]

    def col(*vs):
        return np.stack([np.asarray(v) for v in vs], axis=1)

    arrays = {
        "x": x.reshape(n_tok, P),
        "ctxT": np.asarray(ctx_768).reshape(n_tok // TOK, TOK, CTX).transpose(0, 2, 1),
        "wq1T": np.asarray(L0_xattn_Wq1).T, "wq2T": np.asarray(L0_xattn_Wq2).T,
        "wk1T": np.asarray(L0_xattn_Wk1).T, "wk2T": np.asarray(L0_xattn_Wk2).T,
        "wv1": np.asarray(L0_xattn_Wv1), "wv2": np.asarray(L0_xattn_Wv2),
        "wo1": np.asarray(L0_xattn_Wo1), "wo2": np.asarray(L0_xattn_Wo2),
        "bo1": np.asarray(L0_xattn_bo1), "bo2": np.asarray(L0_xattn_bo2),
        "wp": np.asarray(L0_xattn_Wp), "bp": np.asarray(L0_xattn_bp).reshape(2 * FFC, P).T,
        "w2": np.asarray(L0_xattn_W2), "b2": np.asarray(L0_xattn_b2),
        "ln_g": col(L0_xattn_g1, L0_xattn_g2, L0_xattn_g3),
        "ln_b": col(L0_xattn_be1, L0_xattn_be2, L0_xattn_be3),
    }
    arrays = {f"in_{k}": np.ascontiguousarray(v) for k, v in arrays.items()}
    nc = bacc.Bacc("TRN2", target_bir_lowering=False, num_devices=1)
    d = {k[3:]: nc.dram_tensor(k, v.shape, mybir.dt.from_np(v.dtype), kind="ExternalInput").ap()
         for k, v in arrays.items()}
    out = nc.dram_tensor("out_y", (n_tok, P), F32, kind="ExternalOutput").ap()
    block_kernel(nc, d["x"], d["ctxT"], [d["wq1T"], d["wq2T"]], [d["wk1T"], d["wk2T"]], [d["wv1"], d["wv2"]],
                 [d["wo1"], d["wo2"]], [d["bo1"], d["bo2"]], d["wp"], d["bp"], d["w2"], d["b2"], d["ln_g"],
                 d["ln_b"], out)
    r = run_bass_kernel_spmd(nc, [arrays], core_ids=[0])
    return r.results[0]["out_y"].reshape(x.shape)
```

```python
from contextlib import ExitStack

import concourse.bass as bass
from concourse import mybir

ALU = mybir.AluOpType
ACT = mybir.ActivationFunctionType
F32 = mybir.dt.float32
F32R = mybir.dt.float32r
AX_X = mybir.AxisListType.X

P = 128
SEQ = 64
DH = 64
HEADS = 16
CTX = 96
FF = 512
EPS = 1e-5
SCALE = DH ** -0.5

TOK = 512
PAIRS = TOK // P
HALF = HEADS // 2
HP = HALF // 2
STEPS = 2 * 2 * PAIRS
BLOCKS = STEPS // PAIRS
FFC = FF // P
LN1_AT, LN2_AT, LN3_AT = PAIRS, 2 * PAIRS, 0
FF_AT = PAIRS
GELU_AT = FF_AT + FFC
TURN_BY_DVE = GELU_AT + 1
DOWN_AT = 11


def wait(eng, sem, value):
    if not (isinstance(value, int) and value <= 0):
        eng.wait_ge(sem, value)


def f32(ap):
    return ap.bitcast(F32)


def block_kernel(nc, x, ctxT, wqT, wkT, wv, wo, bo, wp, bp, w2, b2, ln_g, ln_b, out):
    n_tiles = x.shape[0] // TOK
    assert ctxT.shape == (n_tiles, CTX, TOK) and n_tiles >= 4

    with ExitStack() as stack:
        def sb(name, shape, dt=F32):
            return stack.enter_context(nc.sbuf_tensor(name, shape, dt))

        def pb(name, shape):
            return stack.enter_context(nc.psum_tensor(name, shape, F32))

        def sem(name):
            return stack.enter_context(nc.semaphore(name))

        m_hi = [sb(f"m{a}_hi", [P, HEADS, P], F32R) for a in (1, 2)]
        m_lo = [sb(f"m{a}_lo", [P, HEADS, P], F32R) for a in (1, 2)]
        wv_hi = [sb(f"wv{a}_hi", [P, HEADS * DH], F32R) for a in (1, 2)]
        wv_lo = [sb(f"wv{a}_lo", [P, HEADS * DH], F32R) for a in (1, 2)]
        wo_sb = [sb(f"wo{a}_sb", [P, HEADS // 2, P]) for a in (1, 2)]
        wp_hi = sb("wp_hi", [P, 2 * FF], F32R)
        wp_lo = sb("wp_lo", [P, 2 * FF], F32R)
        w2_sb = sb("w2_sb", [P, FFC, P])
        bo_sb = [sb(f"bo{a}_sb", [P, P]) for a in (1, 2)]
        b2_sb = sb("b2_sb", [P, P])
        bp_sb = sb("bp_sb", [P, 2 * FFC])
        g_sb = sb("g_sb", [P, 3])
        be_sb = sb("be_sb", [P, 3])
        ident = sb("ident", [P, P])
        minus_half = sb("minus_half", [P, 1])
        eps_sb = sb("eps_sb", [P, 1])
        table_out = sb("table_out", [P, 1])

        x_in = sb("x_in", [P, PAIRS, P])
        x_bo1 = sb("x_bo1", [P, PAIRS, P])
        x1 = sb("x1", [P, PAIRS, P])
        x1_bo2 = sb("x1_bo2", [P, PAIRS, P])
        x2 = sb("x2", [P, PAIRS, P])
        x2_b2 = sb("x2_b2", [P, PAIRS, P])
        y_out = sb("y_out", [P, PAIRS, P])
        z = sb("z", [P, 2, P])
        stats = sb("stats", [P, 6])
        mean_var = [sb(f"mean_var{k}", [P, 2, 2]) for k in (1, 2, 3)]
        var_eps = [sb(f"var_eps{k}", [P, 2]) for k in (1, 2, 3)]
        rstd = [sb(f"rstd{k}", [P, 2]) for k in (1, 2, 3)]

        h1, h2, h3 = (sb(f"h{k}", [P, TOK]) for k in (1, 2, 3))
        h1_hi, h1_lo = sb("h1_hi", [P, TOK], F32R), sb("h1_lo", [P, TOK], F32R)
        h3_hi, h3_lo = sb("h3_hi", [P, TOK], F32R), sb("h3_lo", [P, TOK], F32R)
        c_in = sb("c_in", [P, TOK])
        c_hi, c_lo = sb("c_hi", [P, TOK], F32R), sb("c_lo", [P, TOK], F32R)
        gate = sb("gate", [P, FFC, TOK])
        up = sb("up", [P, FFC, TOK])

        keys = sb("keys", [P, 2, HALF, TOK])
        values = sb("values", [P, 2, PAIRS, HALF * DH])
        probs = sb("probs", [P, 4, HP, P])
        probsT = sb("probsT", [P, 2, HP, P])
        attnT = sb("attnT", [P, 2, HP, 2, SEQ])
        row_max = sb("row_max", [P, 2, 2 * HP])
        row_sum = sb("row_sum", [P, 2, 2 * HP])
        row_inv = sb("row_inv", [P, 2, 2 * HP])

        scores_ps = pb("scores_ps", [P, 512])
        turn_ps = pb("turn_ps", [P, HP, P])
        attn_ps = pb("attn_ps", [P, 2, 512])
        key_ps = [pb(f"key_ps{i}", [P, 512]) for i in range(2)]
        value_ps = pb("value_ps", [P, 512])
        ln_ps = pb("ln_ps", [P, 512])
        proj_ps = attn_ps[:, 0, 256:384]
        down_ps = ln_ps[:, 256:384]
        last_down_ps = [down_ps, scores_ps[:, 0:P], turn_ps[:, 0, :], value_ps[:, 0:P]]

        W = HEADS * DH
        raw = [keys[:, a, :, :].rearrange("p h t -> p (h t)") for a in (0, 1)]
        wqT_raw = [r[:, 0:W].rearrange("p (c n) -> p c n", n=P) for r in raw]
        cdim = [P, CTX]
        wkT_raw = [r[:, W:W + HEADS // 2 * n].rearrange("p (c n) -> p c n", n=n) for r, n in zip(raw, cdim)]
        wv_raw = [raw[0][:, 2 * W:3 * W], gate[:, :, :].rearrange("p c t -> p (c t)")[:, 0:W]]
        wp_raw = up[:, :, :].rearrange("p c t -> p (c t)")[:, 0:2 * FF]
        banks = [scores_ps[:, :], turn_ps[:, :, :].rearrange("p a b -> p (a b)"), attn_ps[:, 0, :],
                 attn_ps[:, 1, :]]

        qk_loaded = [sem(f"qk_loaded{a}") for a in (1, 2)]
        v_loaded = [sem(f"v_loaded{a}") for a in (1, 2)]
        p_loaded = sem("p_loaded")
        ln_loaded = sem("ln_loaded")
        bo1_loaded = sem("bo1_loaded")
        small_loaded = sem("small_loaded")
        out_w_loaded = sem("out_w_loaded")
        const_made = sem("const_made")
        m_full = sem("m_full")
        w_hi_done = sem("w_hi_done")
        w_lo_done = sem("w_lo_done")
        x_loaded = sem("x_loaded")
        ctx_loaded = sem("ctx_loaded")
        stored = sem("stored")
        stat_done = [sem(f"stat_done{k}") for k in (1, 2, 3)]
        raw_stat = sem("raw_stat")
        eps_added = sem("eps_added")
        rstd_done = [sem(f"rstd_done{k}") for k in (1, 2, 3)]
        z_done = [sem(f"z_done{k}") for k in (1, 2, 3)]
        turned = [sem(f"ln_turned{k}") for k in (1, 2, 3)]
        h_done = [sem(f"h_done{k}") for k in (1, 2, 3)]
        hi_done = [sem(f"hi_done{k}") for k in (1, 2, 3)]
        lo_done = [sem(f"lo_done{k}") for k in (1, 2, 3)]
        c_hi_done = sem("c_hi_done")
        c_lo_done = sem("c_lo_done")
        key_full = sem("key_full")
        key_done = sem("key_done")
        value_full = sem("value_full")
        value_done = sem("value_done")
        scores_full = sem("scores_full")
        max_done = sem("max_done")
        sub_done = sem("sub_done")
        exp_done = sem("exp_done")
        sum_done = sem("sum_done")
        inv_done = sem("inv_done")
        probs_done = sem("probs_done")
        turn_full = sem("turn_full")
        probsT_done = sem("probsT_done")
        attn_full = sem("attn_full")
        attnT_done = sem("attnT_done")
        proj_full = sem("proj_full")
        res_done = sem("res_done")
        x_bo1_done = sem("x_bo1_done")
        x1_bo2_done = sem("x1_bo2_done")
        x2_b2_done = sem("x2_b2_done")
        gate_full = sem("gate_full")
        gate_done = sem("gate_done")
        up_full = sem("up_full")
        up_done = sem("up_done")
        gelu_done = sem("gelu_done")
        gated = sem("gated")
        down_full = sem("down_full")
        out_done = sem("out_done")

        LN, SMALL, OUT_W = 16 * 2, 16 * 3, 16 * 3
        M_BANKS = 4
        WV_PART, WP_PART = [M_BANKS + 1, 2 * M_BANKS + 2], 2 * M_BANKS + 3

        def windows_from_1(eng, window):
            window(1, True, True, True)
            with eng.Fori(2, n_tiles - 1) as T:
                window(T, True, True, True)
            window(n_tiles - 1, True, True, False)
            window(n_tiles, True, False, False)

        FIRST_LN, FIRST_PROJ = range(LN1_AT - 1, LN1_AT + PAIRS + 1), range(STEPS - PAIRS, STEPS)
        FIRST_TURN, FIRST_SPLIT = LN1_AT, LN1_AT + 1
        WV2_AFTER, WP_AFTER = PAIRS - 2, STEPS - 3

        def ln_item(s, prev, cur, nxt):
            for k, at, off, on in ((1, LN1_AT, 1, nxt), (2, LN2_AT, 0, cur), (3, LN3_AT, -1, prev)):
                if on and at <= s < at + PAIRS:
                    return k, s - at, off
            return None

        def ln_item_next(s, prev, cur, nxt):
            if s == STEPS - 1:
                return (3, 0, 0) if cur else None
            return ln_item(s + 1, prev, cur, nxt)

        def eps_count(T, s, prev, cur, nxt):
            in_window = sum(ln_item_next(q, prev, cur, nxt) is not None for q in range(s + 1))
            if isinstance(T, int):
                before = {-1: 0, 0: PAIRS}.get(T, PAIRS + (2 * PAIRS + 1) + 3 * PAIRS * (T - 1))
                if T == n_tiles:
                    before -= PAIRS
            else:
                before = PAIRS + (2 * PAIRS + 1) - 3 * PAIRS + 3 * PAIRS * T
            return before + in_window

        block = stack.enter_context(nc.Block())

        @block.sync
        def _(sp):
            def load_x(t):
                wait(sp, z_done[0], PAIRS * t)
                wait(sp, x_bo1_done, PAIRS * t)
                sp.dma_start(x_in[:, :, :], x[bass.ts(t, TOK), :].rearrange("(c p) d -> p c d", p=P))\
                    .then_inc(x_loaded, 16)

            def load_ctx(t):
                wait(sp, c_lo_done, t)
                sp.dma_start(c_in[0:CTX, :], ctxT[bass.ts(t, 1), :, :].rearrange("a c t -> c (a t)"))\
                    .then_inc(ctx_loaded, 16)

            def store(t):
                sp.wait_ge(out_done, PAIRS * t + PAIRS)
                sp.dma_start(out[bass.ts(t, TOK), :].rearrange("(c p) d -> p c d", p=P), y_out[:, :, :])\
                    .then_inc(stored, 16)

            load_x(0)
            for a in range(2):
                sp.dma_start(wqT_raw[a], wqT[a].rearrange("(c p) n -> p c n", p=P)).then_inc(qk_loaded[a], 16)
                sp.dma_start(wkT_raw[a], wkT[a].rearrange("(c p) n -> p c n", p=P)).then_inc(qk_loaded[a], 16)
                sp.dma_start(wv_raw[a][0:cdim[a], :], wv[a]).then_inc(v_loaded[a], 16)
            load_ctx(0)
            for a in range(2):
                sp.dma_start(wo_sb[a][:, :, :], wo[a].rearrange("(c p) n -> p c n", p=P)).then_inc(out_w_loaded, 16)
            sp.dma_start(w2_sb[:, :, :], w2.rearrange("(c p) n -> p c n", p=P)).then_inc(out_w_loaded, 16)
            sp.dma_start(wp_raw, wp).then_inc(p_loaded, 16)
            load_x(1)
            load_ctx(1)
            with sp.Fori(2, n_tiles) as t:
                load_x(t)
                load_ctx(t)
                store(t - 2)
            store(n_tiles - 2)
            for i in range(PAIRS):
                sp.wait_ge(out_done, PAIRS * (n_tiles - 1) + i + 1)
                rows = (n_tiles - 1) * TOK + i * P
                sp.dma_start(out[rows:rows + P, :], y_out[:, i, :]).then_inc(stored, 16)
            sp.wait_ge(stored, 16 * (n_tiles - 1 + PAIRS))

        @block.gpsimd
        def _(pool):
            pool.memset(minus_half[:, :], -0.5).then_inc(const_made, 1)
            pool.memset(ident[:, :], 0.0).then_inc(const_made, 1)
            pool.memset(eps_sb[:, :], EPS).then_inc(const_made, 1)
            pool.wait_ge(const_made, 3)
            pool.affine_select(out=ident[:, :], in_=ident[:, :], compare_op=ALU.not_equal, fill=1.0, base=0,
                               pattern=[[-1, P]], channel_multiplier=1).then_inc(const_made, 1)
            pool.wait_ge(const_made, 4)

            def window(T, prev, cur, nxt, steps=range(STEPS)):
                for s in steps:
                    G = STEPS * T + s
                    if item := ln_item_next(s, prev, cur, nxt):
                        k, i, off = item
                        n = PAIRS * (T + off) + i
                        wait(pool, stat_done[k - 1], n + 1)
                        slot = i % 2
                        pool.tensor_tensor(var_eps[k - 1][:, slot:slot + 1], mean_var[k - 1][:, slot, 1:2],
                                           eps_sb[:, :], ALU.add).then_inc(eps_added, 1)
                        wait(pool, eps_added, eps_count(T, s, prev, cur, nxt))
                        pool.tensor_tensor(rstd[k - 1][:, slot:slot + 1], var_eps[k - 1][:, slot:slot + 1],
                                           minus_half[:, :], ALU.pow).then_inc(rstd_done[k - 1], 1)
                    if prev and s < PAIRS:
                        n = PAIRS * (T - 1) + s
                        cols = slice(s * P, (s + 1) * P)
                        wait(pool, hi_done[2], n + 1)
                        pool.tensor_tensor(h3_lo[:, cols], h3[:, cols], f32(h3_hi[:, cols]), ALU.subtract)\
                            .then_inc(lo_done[2], 1)
                        wait(pool, res_done, STEPS * (T - 1) + 3 * PAIRS + s + 1)
                        pool.tensor_tensor(x2_b2[:, s, :], x2[:, s, :], b2_sb[:, :], ALU.add)\
                            .then_inc(x2_b2_done, 1)
                    if nxt and LN1_AT <= s < LN1_AT + PAIRS:
                        i = s - LN1_AT
                        if isinstance(T, int) and T == -1 and i == 0:
                            pool.wait_ge(bo1_loaded, 16)
                        wait(pool, x_loaded, 16 * (T + 2))
                        wait(pool, res_done, STEPS * T + i + 1)
                        pool.tensor_tensor(x_bo1[:, i, :], x_in[:, i, :], bo_sb[0][:, :], ALU.add)\
                            .then_inc(x_bo1_done, 1)
                    if nxt and LN1_AT < s <= LN1_AT + PAIRS:
                        i = s - LN1_AT - 1
                        cols = slice(i * P, (i + 1) * P)
                        wait(pool, hi_done[0], PAIRS * (T + 1) + i + 1)
                        pool.tensor_tensor(h1_lo[:, cols], h1[:, cols], f32(h1_hi[:, cols]), ALU.subtract)\
                            .then_inc(lo_done[0], 1)
                    if cur and s == 2:
                        wait(pool, c_hi_done, T + 1)
                        pool.tensor_tensor(c_lo[0:CTX, :], c_in[0:CTX, :], f32(c_hi[0:CTX, :]), ALU.subtract)\
                            .then_inc(c_lo_done, 1)
                    if cur and LN2_AT <= s < LN2_AT + PAIRS:
                        i = s - LN2_AT
                        wait(pool, res_done, STEPS * T + PAIRS + i + 1)
                        pool.tensor_tensor(x1_bo2[:, i, :], x1[:, i, :], bo_sb[1][:, :], ALU.add)\
                            .then_inc(x1_bo2_done, 1)
                    if prev and cur and GELU_AT < s <= GELU_AT + 2:
                        wait(pool, gelu_done, T)
                        wait(pool, up_done, FFC * T)
                        for j in range(2 * (s - GELU_AT - 1), 2 * (s - GELU_AT)):
                            pool.tensor_tensor(up[:, j, :], up[:, j, :], gate[:, j, :], ALU.mult)\
                                .then_inc(gated, 1)

            window(-1, False, False, True, FIRST_LN)
            pool.wait_ge(small_loaded, SMALL)
            window(0, False, True, True)
            windows_from_1(pool, window)

        @block.scalar
        def _(act):
            act.dma_start(g_sb[:, :], ln_g).then_inc(ln_loaded, 16)
            act.dma_start(be_sb[:, :], ln_b).then_inc(ln_loaded, 16)
            act.dma_start(bo_sb[0][:, :], bo[0].partition_broadcast(P)).then_inc(bo1_loaded, 16)
            act.wait_ge(const_made, 1)
            act.activation(table_out[:, :], minus_half[:, :], ACT.Copy)
            act.dma_start(bp_sb[:, :], bp).then_inc(small_loaded, 16)
            for dst, src in ((bo_sb[1], bo[1]), (b2_sb, b2)):
                act.dma_start(dst[:, :], src.partition_broadcast(P)).then_inc(small_loaded, 16)

            def m_high_part(a, n):
                heads = m_hi[a][0:cdim[a], :, :].rearrange("p (c q) n -> p c q n", q=2)
                par, c = n // 2, n % 2
                act.wait_ge(m_full, M_BANKS * a + n + 1)
                act.activation(heads[:, 4 * c:4 * c + 4, par, :],
                               banks[n][0:cdim[a], :].rearrange("p (c n) -> p c n", n=P),
                               ACT.Copy, scale=SCALE).then_inc(w_hi_done, 1)

            def wv_high_part(a):
                act.wait_ge(v_loaded[a], 16)
                act.activation(wv_hi[a][0:cdim[a], :], wv_raw[a][0:cdim[a], :], ACT.Copy).then_inc(w_hi_done, 1)

            def window(T, prev, cur, nxt, steps=range(STEPS)):
                for s in steps:
                    G = STEPS * T + s
                    lagged = cur if s >= 2 else prev
                    if lagged and s != TURN_BY_DVE:
                        wait(act, turn_full, G - 1)
                        wait(act, attn_full, G - 3)
                        act.activation(probsT[:, s % 2, :, :], turn_ps[:, :, :], ACT.Copy)\
                            .then_inc(probsT_done, 1)
                    j = G + PAIRS
                    projecting = cur if s < STEPS - PAIRS else nxt
                    buf = (s // PAIRS + 1) % 2

                    def key_copy(u):
                        wait(act, key_full, 2 * j + u + 1)
                        act.activation(keys[:, buf, 2 * (s % PAIRS) + u, :], key_ps[u][:, :], ACT.Copy)\
                            .then_inc(key_done, 1)

                    if projecting:
                        if s % PAIRS == 0:
                            wait(act, scores_full, j - PAIRS)
                        key_copy(0)
                    if prev and s < PAIRS:
                        cols = slice(s * P, (s + 1) * P)
                        wait(act, h_done[2], PAIRS * (T - 1) + s + 1)
                        act.activation(h3_hi[:, cols], h3[:, cols], ACT.Copy).then_inc(hi_done[2], 1)
                    if nxt and LN1_AT < s <= LN1_AT + PAIRS:
                        i = s - LN1_AT - 1
                        cols = slice(i * P, (i + 1) * P)
                        wait(act, h_done[0], PAIRS * (T + 1) + i + 1)
                        act.activation(h1_hi[:, cols], h1[:, cols], ACT.Copy).then_inc(hi_done[0], 1)
                    if lagged:
                        wait(act, attn_full, G - 1)
                        wait(act, proj_full, G - 3)
                        act.activation(attnT[:, s % 2, :, :, :].rearrange("p h b q -> p b h q"),
                                       attn_ps[:, :, 0:HP * SEQ].rearrange("p b (h q) -> p b h q", q=SEQ),
                                       ACT.Copy).then_inc(attnT_done, 1)
                    if projecting:
                        key_copy(1)
                        wait(act, value_full, j + 1)
                        wait(act, attn_full, j - 2 * PAIRS + 1)
                        act.activation(values[:, buf, s % PAIRS, :], value_ps[:, :], ACT.Copy)\
                            .then_inc(value_done, 1)
                    if cur:
                        wait(act, sub_done, G + 1)
                        e = probs[:, s % 4, :, :]
                        act.activation(e, e, ACT.Exp).then_inc(exp_done, 1)
                    if cur and s == 1:
                        wait(act, ctx_loaded, 16 * (T + 1))
                        act.activation(c_hi[0:CTX, :], c_in[0:CTX, :], ACT.Copy).then_inc(c_hi_done, 1)
                    if prev and FF_AT <= s < FF_AT + FFC:
                        i = s - FF_AT
                        wait(act, gate_full, FFC * (T - 1) + i + 1)
                        wait(act, gated, FFC * (T - 1))
                        act.activation(gate[:, i, :], key_ps[0][:, :], ACT.Identity if cur else ACT.Gelu,
                                       bias=bp_sb[:, FFC + i:FFC + i + 1]).then_inc(gate_done, 1)
                    if prev and cur and s == GELU_AT:
                        wait(act, gate_done, FFC * T)
                        act.activation(gate[:, :, :], gate[:, :, :], ACT.Gelu).then_inc(gelu_done, 1)

            for s in FIRST_LN:
                window(-1, False, False, True, (s,))
                if s >= FIRST_SPLIT:
                    m_high_part(0, s - FIRST_SPLIT)
            wv_high_part(0)
            for n in range(M_BANKS):
                m_high_part(1, n)
            window(-1, False, False, True, FIRST_PROJ)
            for s in range(STEPS):
                window(0, False, True, True, (s,))
                if s == WV2_AFTER:
                    wv_high_part(1)
                if s == WP_AFTER:
                    act.wait_ge(p_loaded, 16)
                    act.activation(wp_hi[:, :], wp_raw, ACT.Copy).then_inc(w_hi_done, 1)
            act.wait_ge(small_loaded, SMALL)
            windows_from_1(act, window)

        @block.vector
        def _(dve):
            def low_part(n, dst, src, hi, rows):
                dve.wait_ge(w_hi_done, n)
                dve.tensor_tensor(dst[0:rows, :], src[0:rows, :], f32(hi[0:rows, :]), ALU.subtract)\
                    .then_inc(w_lo_done, 1)

            def m_low_part(a, n):
                hi = f32(m_hi[a][0:cdim[a], :, :]).rearrange("p (c q) n -> p c q n", q=2)
                lo = m_lo[a][0:cdim[a], :, :].rearrange("p (c q) n -> p c q n", q=2)
                par, c = n // 2, n % 2
                dve.wait_ge(w_hi_done, (M_BANKS + 1) * a + n + 1)
                dve.scalar_tensor_tensor(out=lo[:, 4 * c:4 * c + 4, par, :],
                                         in0=banks[n][0:cdim[a], :].rearrange("p (c n) -> p c n", n=P),
                                         scalar=SCALE, in1=hi[:, 4 * c:4 * c + 4, par, :],
                                         op0=ALU.mult, op1=ALU.subtract).then_inc(w_lo_done, 1)

            def wv_low_part(a):
                low_part(WV_PART[a], wv_lo[a], wv_raw[a], wv_hi[a], cdim[a])

            def ln_out(k, i, off, T, h):
                wait(dve, turned[k - 1], PAIRS * (T + off) + i + 1)
                dve.tensor_scalar(h[:, i * P:(i + 1) * P], ln_ps[:, 0:P], g_sb[:, k - 1:k], be_sb[:, k - 1:k],
                                  ALU.mult, ALU.add).then_inc(h_done[k - 1], 1)

            def window(T, prev, cur, nxt, steps=range(STEPS)):
                for s in steps:
                    G = STEPS * T + s
                    if cur if s >= 3 else prev:
                        q = (s - 3) % STEPS
                        t = T if s >= 3 else T - 1
                        i = q % PAIRS
                        wait(dve, proj_full, G - 2)
                        if q // PAIRS == 0:
                            wait(dve, x_bo1_done, PAIRS * t + i + 1)
                            wait(dve, x1_bo2_done, PAIRS * (t - 1) + i + 1)
                            dst, src = x1[:, i, :], x_bo1[:, i, :]
                        elif q // PAIRS == 1:
                            dst, src = x1[:, i, :], x1[:, i, :]
                        elif q // PAIRS == 2:
                            wait(dve, x1_bo2_done, PAIRS * t + i + 1)
                            wait(dve, x2_b2_done, PAIRS * (t - 1) + i + 1)
                            dst, src = x2[:, i, :], x1_bo2[:, i, :]
                        else:
                            dst, src = x2[:, i, :], x2[:, i, :]
                        if q // PAIRS % 2:
                            wait(dve, res_done, G - 3 - PAIRS + 1)
                        dve.tensor_tensor(dst, proj_ps, src, ALU.add).then_inc(res_done, 1)
                    if prev and not cur and s == FF_AT + FFC:
                        for i in range(PAIRS):
                            wait(dve, down_full, PAIRS * (T - 1) + i + 1)
                            if i == 0:
                                wait(dve, x2_b2_done, PAIRS * T)
                                wait(dve, stored, 16 * (T - 1))
                            dve.tensor_tensor(y_out[:, i, :], last_down_ps[i], x2_b2[:, i, :], ALU.add)\
                                .then_inc(out_done, 1)
                    if prev and cur and DOWN_AT < s <= DOWN_AT + PAIRS:
                        i = s - DOWN_AT - 1
                        wait(dve, down_full, PAIRS * (T - 1) + i + 1)
                        wait(dve, x2_b2_done, PAIRS * (T - 1) + i + 1)
                        if i == 0:
                            wait(dve, stored, 16 * (T - 1))
                        dve.tensor_tensor(y_out[:, i, :], down_ps, x2_b2[:, i, :], ALU.add).then_inc(out_done, 1)
                    item = ln_item(s, prev, cur, nxt)
                    if item and item[0] != 1:
                        ln_out(*item, T, h2 if item[0] == 2 else h3)
                    after = ln_item_next(s, prev, cur, nxt)
                    if after:
                        k, i, off = after
                        n = PAIRS * (T + off) + i
                        src = (x_in, x1, x2)[k - 1][:, i, :]
                        if k == 1:
                            wait(dve, x_loaded, 16 * (T + 2))
                        else:
                            wait(dve, res_done, G - 2)
                        dve.bn_stats(stats[:, :], src).then_inc(raw_stat, 1)
                    if cur and s == TURN_BY_DVE:
                        wait(dve, turn_full, G - 1)
                        wait(dve, attn_full, G - 3)
                        dve.tensor_copy(probsT[:, s % 2, :, :], turn_ps[:, :, :]).then_inc(probsT_done, 1)
                    if cur if s >= 1 else prev:
                        e = probs[:, (s - 1) % 4, :, :].rearrange("p h (b k) -> p (h b) k", k=SEQ)
                        r = (s - 1) % 2
                        wait(dve, exp_done, G)
                        if after:
                            wait(dve, raw_stat, eps_count(T, s, prev, cur, nxt))
                        dve.tensor_reduce(row_sum[:, r, :], e, AX_X, ALU.add).then_inc(sum_done, 1)
                    elif after:
                        wait(dve, raw_stat, eps_count(T, s, prev, cur, nxt))
                    if after:
                        dve.bn_aggr(mean_var[k - 1][:, i % 2, :], stats[:, :]).then_inc(stat_done[k - 1], 1)
                    if cur if s >= 1 else prev:
                        wait(dve, sum_done, G)
                        dve.reciprocal(row_inv[:, r, :], row_sum[:, r, :]).then_inc(inv_done, 1)
                        wait(dve, inv_done, G)
                        dve.tensor_tensor(e, e, row_inv[:, r, :].unsqueeze(2).to_broadcast([P, 2 * HP, SEQ]),
                                          ALU.mult).then_inc(probs_done, 1)
                    if after:
                        wait(dve, rstd_done[k - 1], n + 1)
                        if i >= 2:
                            wait(dve, turned[k - 1], n - 1)
                        dve.tensor_scalar(z[:, i % 2, :], src, mean_var[k - 1][:, i % 2, 0:1],
                                          rstd[k - 1][:, i % 2:i % 2 + 1], ALU.subtract, ALU.mult)\
                            .then_inc(z_done[k - 1], 1)
                    if cur:
                        sc = scores_ps[:, :].rearrange("p (g k) -> p g k", k=SEQ)
                        e = probs[:, s % 4, :, :].rearrange("p h (b k) -> p (h b) k", k=SEQ)
                        r = s % 2
                        wait(dve, scores_full, G + 1)
                        dve.tensor_reduce(row_max[:, r, :], sc, AX_X, ALU.max).then_inc(max_done, 1)
                        wait(dve, max_done, G + 1)
                        wait(dve, turn_full, G - 3)
                        dve.tensor_tensor(e, sc, row_max[:, r, :].unsqueeze(2).to_broadcast([P, 2 * HP, SEQ]),
                                          ALU.subtract).then_inc(sub_done, 1)
                    if item and item[0] == 1:
                        ln_out(*item, T, h1)
                    if prev and FF_AT <= s < FF_AT + FFC:
                        i = s - FF_AT
                        wait(dve, up_full, FFC * (T - 1) + i + 1)
                        if cur:
                            dve.tensor_scalar(up[:, i, :], key_ps[1][:, :], bp_sb[:, i:i + 1], None, ALU.add)\
                                .then_inc(up_done, 1)
                        else:
                            wait(dve, gate_done, FFC * (T - 1) + i + 1)
                            dve.scalar_tensor_tensor(out=up[:, i, :], in0=key_ps[1][:, :],
                                                     scalar=bp_sb[:, i:i + 1], in1=gate[:, i, :], op0=ALU.add,
                                                     op1=ALU.mult).then_inc(up_done, 1)

            for s in FIRST_LN:
                if s == FIRST_TURN:
                    dve.wait_ge(ln_loaded, LN)
                window(-1, False, False, True, (s,))
                if s >= FIRST_SPLIT:
                    m_low_part(0, s - FIRST_SPLIT)
            wv_low_part(0)
            for n in range(M_BANKS):
                m_low_part(1, n)
            for s in range(STEPS):
                window(0, False, True, True, (s,))
                if s == WV2_AFTER:
                    wv_low_part(1)
                if s == WP_AFTER:
                    low_part(WP_PART, wp_lo, wp_raw, wp_hi, P)
            dve.wait_ge(small_loaded, SMALL)
            windows_from_1(dve, window)

        @block.tensor
        def _(pe):
            def build_m(a, n):
                par, c = n // 2, n % 2
                rows = slice(par * DH, (par + 1) * DH)
                pe.wait_ge(qk_loaded[a], 32)
                if a == 1:
                    pe.wait_ge(w_lo_done, n + 1)
                for q in range(4):
                    mm = pe.matmul(banks[n][0:cdim[a], q * P:(q + 1) * P], wkT_raw[a][rows, 4 * c + q, :],
                                   wqT_raw[a][rows, 4 * c + q, :], start=True, stop=True)
                mm.then_inc(m_full, 1)

            def split_product(dst, w_hi, w_lo, v_hi, v_lo):
                pe.matmul(dst, w_hi, v_hi, start=True, stop=False)
                pe.matmul(dst, w_hi, v_lo, start=False, stop=False)
                return pe.matmul(dst, w_lo, v_hi, start=False, stop=True)

            def attn_waits(G):
                wait(pe, probsT_done, G - 1)
                wait(pe, value_done, G - 1)
                wait(pe, attnT_done, G - 2)
                wait(pe, res_done, G - 2)

            def window(T, prev, cur, nxt, steps=range(STEPS)):
                for s in steps:
                    G = STEPS * T + s
                    item = ln_item(s, prev, cur, nxt)
                    if item:
                        k, i, off = item
                        n = PAIRS * (T + off) + i
                        wait(pe, z_done[k - 1], n + 1)
                        if i > 0:
                            wait(pe, h_done[k - 1], n)
                        elif k == 3:
                            wait(pe, h_done[1], PAIRS * T)
                            wait(pe, out_done, PAIRS * (T - 1))
                        elif k == 2 and nxt:
                            wait(pe, h_done[0], PAIRS * (T + 2))
                        else:
                            wait(pe, h_done[2], PAIRS * T)
                        pe.transpose(ln_ps[:, 0:P], z[:, i % 2, :], ident[:, :]).then_inc(turned[k - 1], 1)
                    lagged = cur if s >= 2 else prev
                    if lagged:
                        wait(pe, probs_done, G - 1)
                        wait(pe, probsT_done, G - 2)
                        for hp in range(HP):
                            mm = pe.transpose(turn_ps[:, hp, :], probs[:, (s - 2) % 4, hp, :], ident[:, :])
                        mm.then_inc(turn_full, 1)
                    j = G + PAIRS
                    projecting = cur if s < STEPS - PAIRS else nxt
                    nb = (s // PAIRS + 1) % BLOCKS
                    a, half = nb // 2, nb % 2
                    rows = cdim[a]
                    src_hi, src_lo = ((h1_hi, h1_lo), (c_hi, c_lo))[a]

                    def key_unit(u):
                        head = half * HALF + 2 * (s % PAIRS) + u
                        wait(pe, key_done, 2 * j + u - 1)
                        if prev and FF_AT < s <= FF_AT + FFC:
                            wait(pe, (gate_done, up_done)[u], FFC * (T - 1) + s - FF_AT)
                        split_product(key_ps[u][:, :], m_hi[a][0:rows, head, :], m_lo[a][0:rows, head, :],
                                      src_hi[0:rows, :], src_lo[0:rows, :]).then_inc(key_full, 1)

                    if projecting:
                        if s == STEPS - PAIRS:
                            wait(pe, lo_done[0], PAIRS * (T + 2))
                        if s == PAIRS:
                            wait(pe, c_lo_done, T + 1)
                        key_unit(0)
                    if cur:
                        blk, i = s // PAIRS, s % PAIRS
                        if i == 0:
                            wait(pe, key_done, 2 * (G + PAIRS))
                        h = h1 if blk < 2 else h2
                        if blk == 2:
                            wait(pe, h_done[1], PAIRS * T + i + 1)
                        wait(pe, sub_done, G)
                        dst = scores_ps[:, :].rearrange("p (h b k) -> p h b k", b=2, k=SEQ)
                        by_head = keys[:, blk % 2, :, :].rearrange("p (h q) t -> p h q t", q=2)
                        for b in range(2):
                            cols = slice(i * P + b * SEQ, i * P + (b + 1) * SEQ)
                            for par in range(2):
                                if lagged and (b, par) == (1, 1):
                                    attn_waits(G)
                                mm = pe.matmul(dst[par * SEQ:(par + 1) * SEQ, :, b, :], h[:, cols],
                                               by_head[:, :, par, cols], start=True, stop=True)
                        mm.then_inc(scores_full, 1)
                    if lagged:
                        buf = (s - 2) % STEPS // PAIRS % 2
                        pair = (s - 2) % PAIRS
                        if not cur:
                            attn_waits(G)
                        for hp in range(HP):
                            for b, par in ((0, 0), (1, 1), (1, 0), (0, 1)):
                                keys_of = slice(b * SEQ, (b + 1) * SEQ)
                                h = 2 * hp + par
                                mm = pe.matmul(attn_ps[par * DH:(par + 1) * DH, b, hp * SEQ:(hp + 1) * SEQ],
                                               values[keys_of, buf, pair, h * DH:(h + 1) * DH],
                                               probsT[keys_of, s % 2, hp, par * SEQ:(par + 1) * SEQ],
                                               start=True, stop=True)
                        mm.then_inc(attn_full, 1)
                    if projecting:
                        key_unit(1)
                        tok = slice(s % PAIRS * P, (s % PAIRS + 1) * P)
                        cols = slice(half * HALF * DH, (half + 1) * HALF * DH)
                        wait(pe, value_done, j)
                        split_product(value_ps[:, :], src_hi[0:rows, tok], src_lo[0:rows, tok],
                                      wv_hi[a][0:rows, cols], wv_lo[a][0:rows, cols]).then_inc(value_full, 1)
                    if prev and FF_AT <= s < FF_AT + FFC:
                        i = s - FF_AT
                        if i == 0:
                            wait(pe, lo_done[2], PAIRS * T)
                        for u, c, full, done in ((0, FFC + i, gate_full, gate_done), (1, i, up_full, up_done)):
                            wait(pe, key_done, 2 * j + u + 1 if cur else 2 * STEPS * n_tiles)
                            wait(pe, done, FFC * (T - 1) + i)
                            ps = key_ps[u]
                            cols = slice(c * P, (c + 1) * P)
                            split_product(ps[:, :], wp_hi[:, cols], wp_lo[:, cols], h3_hi[:, :], h3_lo[:, :])\
                                .then_inc(full, 1)
                    if prev and not cur and FF_AT < s <= FF_AT + FFC:
                        i = s - FF_AT - 1
                        if i == 0:
                            wait(pe, h_done[2], PAIRS * T)
                            wait(pe, sub_done, STEPS * T)
                            wait(pe, probsT_done, STEPS * T)
                            wait(pe, value_done, STEPS * T)
                        wait(pe, up_done, FFC * (T - 1) + i + 1)
                        for p in range(PAIRS):
                            mm = pe.matmul(last_down_ps[p], up[:, i, p * P:(p + 1) * P], w2_sb[:, i, :],
                                           start=(i == 0), stop=(i == FFC - 1))
                            if i == FFC - 1:
                                mm.then_inc(down_full, 1)
                    if prev and cur and DOWN_AT <= s < DOWN_AT + PAIRS:
                        i = s - DOWN_AT
                        if i == 0:
                            wait(pe, gated, FFC * T)
                            wait(pe, h_done[1], PAIRS * (T + 1))
                        wait(pe, out_done, PAIRS * (T - 1) + i)
                        for c in range(FFC):
                            mm = pe.matmul(down_ps, up[:, c, i * P:(i + 1) * P], w2_sb[:, c, :],
                                           start=(c == 0), stop=(c == FFC - 1))
                        mm.then_inc(down_full, 1)
                    if lagged:
                        blk = (s - 2) % STEPS // PAIRS
                        wait(pe, attnT_done, G - 1)
                        for hp in range(HP):
                            mm = pe.matmul(proj_ps, attnT[:, s % 2, hp, :, :].rearrange("p b q -> p (b q)"),
                                           wo_sb[blk // 2][:, blk % 2 * HP + hp, :],
                                           start=(hp == 0), stop=(hp == HP - 1))
                        mm.then_inc(proj_full, 1)

            pe.wait_ge(const_made, 4)
            for n in range(M_BANKS):
                window(-1, False, False, True, (FIRST_TURN + n,))
                build_m(0, n)
            for n in range(M_BANKS):
                build_m(1, n)
            pe.wait_ge(w_lo_done, WV_PART[0])
            window(-1, False, False, True, FIRST_PROJ)
            pe.wait_ge(w_lo_done, WV_PART[1] - 1)
            pe.wait_ge(out_w_loaded, OUT_W)
            window(0, False, True, True, range(PAIRS))
            pe.wait_ge(w_lo_done, WV_PART[1])
            window(0, False, True, True, range(PAIRS, STEPS))
            pe.wait_ge(w_lo_done, WP_PART)
            windows_from_1(pe, window)


def kernel(x, ctx_768, L0_xattn_Wq1, L0_xattn_Wk1, L0_xattn_Wv1, L0_xattn_Wo1, L0_xattn_bo1, L0_xattn_Wq2,
           L0_xattn_Wk2, L0_xattn_Wv2, L0_xattn_Wo2, L0_xattn_bo2, L0_xattn_Wp, L0_xattn_bp, L0_xattn_W2,
           L0_xattn_b2, L0_xattn_g1, L0_xattn_be1, L0_xattn_g2, L0_xattn_be2, L0_xattn_g3, L0_xattn_be3):
    import numpy as np
    import concourse.bacc as bacc
    from concourse.bass_utils import run_bass_kernel_spmd

    x = np.asarray(x)
    n_tok = x.shape[0] * x.shape[1]

    def col(*vs):
        return np.stack([np.asarray(v) for v in vs], axis=1)

    arrays = {
        "x": x.reshape(n_tok, P),
        "ctxT": np.asarray(ctx_768).reshape(n_tok // TOK, TOK, CTX).transpose(0, 2, 1),
        "wq1T": np.asarray(L0_xattn_Wq1).T, "wq2T": np.asarray(L0_xattn_Wq2).T,
        "wk1T": np.asarray(L0_xattn_Wk1).T, "wk2T": np.asarray(L0_xattn_Wk2).T,
        "wv1": np.asarray(L0_xattn_Wv1), "wv2": np.asarray(L0_xattn_Wv2),
        "wo1": np.asarray(L0_xattn_Wo1), "wo2": np.asarray(L0_xattn_Wo2),
        "bo1": np.asarray(L0_xattn_bo1), "bo2": np.asarray(L0_xattn_bo2),
        "wp": np.asarray(L0_xattn_Wp), "bp": np.asarray(L0_xattn_bp).reshape(2 * FFC, P).T,
        "w2": np.asarray(L0_xattn_W2), "b2": np.asarray(L0_xattn_b2),
        "ln_g": col(L0_xattn_g1, L0_xattn_g2, L0_xattn_g3),
        "ln_b": col(L0_xattn_be1, L0_xattn_be2, L0_xattn_be3),
    }
    arrays = {f"in_{k}": np.ascontiguousarray(v) for k, v in arrays.items()}
    nc = bacc.Bacc("TRN2", target_bir_lowering=False, num_devices=1)
    d = {k[3:]: nc.dram_tensor(k, v.shape, mybir.dt.from_np(v.dtype), kind="ExternalInput").ap()
         for k, v in arrays.items()}
    out = nc.dram_tensor("out_y", (n_tok, P), F32, kind="ExternalOutput").ap()
    block_kernel(nc, d["x"], d["ctxT"], [d["wq1T"], d["wq2T"]], [d["wk1T"], d["wk2T"]], [d["wv1"], d["wv2"]],
                 [d["wo1"], d["wo2"]], [d["bo1"], d["bo2"]], d["wp"], d["bp"], d["w2"], d["b2"], d["ln_g"],
                 d["ln_b"], out)
    r = run_bass_kernel_spmd(nc, [arrays], core_ids=[0])
    return r.results[0]["out_y"].reshape(x.shape)
```
